# Optimizing a Trainium2 kernel written in Bass

```python
import numpy as np
import jax
import jax.numpy as jnp

def _softmax(x, axis=-1):
    return jax.nn.softmax(x, axis=axis)

def _gelu(x):
    return jax.nn.gelu(x, approximate=True)

def _silu(x):
    return jax.nn.silu(x)

def _sigmoid(x):
    return jax.nn.sigmoid(x)

def _layernorm(x, axis=-1, eps=1e-05):
    m = jnp.mean(x, axis=axis, keepdims=True)
    v = jnp.var(x, axis=axis, keepdims=True)
    return (x - m) / jnp.sqrt(v + eps)

def _scatter_add(tgt, idx, src, axis=0):
    return tgt.at[idx].add(src)

def _segment_sum(src, seg, n):
    return jax.ops.segment_sum(src, seg, n)
kernel_name = 'mk_seq_postln_d1_jaxref_r4_864b27'

def setup_inputs(seed: int=0):
    np.random.seed(seed)
    _w = jnp.asarray

    def _L0_attn_setup():
        import jax, jax.numpy as jnp
        import numpy as np
        B, L, DM = (4, 512, 256)
        key = jax.random.key(seed)
        ks = jax.random.split(key, 13)
        n = lambda k, shape, s=1.0: jax.random.normal(k, shape, dtype=jnp.float32) * s
        W_SCALE = 0.02
        K_SCALE = 0.02
        return {'u': n(ks[0], (B, L, DM)), 'Wq': n(ks[1], (DM, DM), W_SCALE), 'bq': n(ks[2], (DM,), W_SCALE), 'Wk': n(ks[3], (DM, DM), W_SCALE), 'bk': n(ks[4], (DM,), W_SCALE), 'Wv': n(ks[5], (DM, DM), W_SCALE), 'bv': n(ks[6], (DM,), W_SCALE), 'k_kernel': n(ks[7], (DM, L), K_SCALE), 'k_D': n(ks[8], (DM,)), 'ssm_kernel': n(ks[9], (DM, L), K_SCALE), 'D': n(ks[10], (DM,)), 'Wo': n(ks[11], (DM, DM), W_SCALE), 'bo': n(ks[12], (DM,), W_SCALE)}
    _L0_attn_in = _L0_attn_setup()

    def _L0_ffn_setup():
        import jax, jax.numpy as jnp
        import numpy as np
        import math
        BETA = 0.9
        THRESHOLD = 1.0
        NUM_STEPS = 5
        ALPHA = 2.0

        @jax.custom_vjp
        def spike_fn(u):
            return (u > 0).astype(u.dtype)

        def _spike_fwd(u):
            return (spike_fn(u), u)

        def _spike_bwd(u, g):
            s = jnp.pi / 2.0 * ALPHA * u
            return (g * (ALPHA / 2.0) / (1.0 + s * s),)
        spike_fn.defvjp(_spike_fwd, _spike_bwd)
        key = jax.random.key(seed)
        k1, k2, k3 = jax.random.split(key, 3)
        n_embd = 256
        x = jax.random.normal(k1, (4, 512, n_embd), dtype=jnp.float32)
        W_fc = jax.random.normal(k2, (4 * n_embd, n_embd), dtype=jnp.float32) / math.sqrt(n_embd)
        W_proj = jax.random.normal(k3, (n_embd, 4 * n_embd), dtype=jnp.float32) / math.sqrt(4 * n_embd)
        return {'x': x, 'W_fc': W_fc, 'W_proj': W_proj}
    _L0_ffn_in = _L0_ffn_setup()
    _d = {'L0_attn_u': _L0_attn_in['u'], 'L0_attn_Wq': _L0_attn_in['Wq'], 'L0_attn_bq': _L0_attn_in['bq'], 'L0_attn_Wk': _L0_attn_in['Wk'], 'L0_attn_bk': _L0_attn_in['bk'], 'L0_attn_Wv': _L0_attn_in['Wv'], 'L0_attn_bv': _L0_attn_in['bv'], 'L0_attn_k_kernel': _L0_attn_in['k_kernel'], 'L0_attn_k_D': _L0_attn_in['k_D'], 'L0_attn_ssm_kernel': _L0_attn_in['ssm_kernel'], 'L0_attn_D': _L0_attn_in['D'], 'L0_attn_Wo': _L0_attn_in['Wo'], 'L0_attn_bo': _L0_attn_in['bo'], 'L0_ffn_W_fc': _L0_ffn_in['W_fc'], 'L0_ffn_W_proj': _L0_ffn_in['W_proj']}
    _x0 = _d['L0_attn_u']
    _d['L0_attn_u'] = jax.random.normal(jax.random.fold_in(jax.random.key(seed), 1), (16, 512, 256), dtype=_x0.dtype)
    del _x0
    return _d

def reference(L0_attn_u, L0_attn_Wq, L0_attn_bq, L0_attn_Wk, L0_attn_bk, L0_attn_Wv, L0_attn_bv, L0_attn_k_kernel, L0_attn_k_D, L0_attn_ssm_kernel, L0_attn_D, L0_attn_Wo, L0_attn_bo, L0_ffn_W_fc, L0_ffn_W_proj):

    def _L0_attn_ref(u, Wq, bq, Wk, bk, Wv, bv, k_kernel, k_D, ssm_kernel, D, Wo, bo):
        import jax, jax.numpy as jnp
        import numpy as np
        B, L, DM = (4, 512, 256)
        Lseq = u.shape[1]
        fft_size = 2 * Lseq
        q = jnp.einsum('blh,dh->bdl', u, Wq) + bq[None, :, None]
        k = jnp.einsum('blh,dh->bdl', u, Wk) + bk[None, :, None]
        v = jnp.einsum('blh,dh->bdl', u, Wv) + bv[None, :, None]
        k_kernel_f = jnp.fft.rfft(k_kernel, n=fft_size)
        k_f = jnp.fft.rfft(k, n=fft_size)
        shift_k = jnp.fft.irfft(k_kernel_f[None] * k_f, n=fft_size)[..., :Lseq]
        k = shift_k + k_D[None, :, None] * k
        kv = k * v
        kv_f = jnp.fft.rfft(kv, n=fft_size)
        ssm_kernel_f = jnp.fft.rfft(ssm_kernel, n=fft_size)
        y = jnp.fft.irfft(kv_f * ssm_kernel_f[None], n=fft_size)[..., :Lseq]
        y = y + kv * D[None, :, None]
        y = y * q
        y = jnp.swapaxes(y, 1, 2)
        return jnp.einsum('blh,oh->blo', y, Wo) + bo

    def _L0_ffn_ref(x, W_fc, W_proj):
        import jax, jax.numpy as jnp
        import numpy as np
        import math
        BETA = 0.9
        THRESHOLD = 1.0
        NUM_STEPS = 5
        ALPHA = 2.0

        @jax.custom_vjp
        def spike_fn(u):
            return (u > 0).astype(u.dtype)

        def _spike_fwd(u):
            return (spike_fn(u), u)

        def _spike_bwd(u, g):
            s = jnp.pi / 2.0 * ALPHA * u
            return (g * (ALPHA / 2.0) / (1.0 + s * s),)
        spike_fn.defvjp(_spike_fwd, _spike_bwd)
        h = jnp.square(jax.nn.relu(jnp.einsum('bsd,fd->bsf', x, W_fc)))
        y = jnp.einsum('bsf,df->bsd', h, W_proj)

        def step(mem, _):
            reset = jax.lax.stop_gradient(spike_fn(mem - THRESHOLD))
            mem_new = BETA * mem + y - reset * THRESHOLD
            spk = spike_fn(mem_new - THRESHOLD)
            return (mem_new, spk)
        mem0 = jnp.zeros_like(y)
        _, spks = jax.lax.scan(step, mem0, None, length=NUM_STEPS)
        return jnp.sum(spks, axis=0) / NUM_STEPS
    x = L0_attn_u
    x = _layernorm(x + _L0_attn_ref(x, L0_attn_Wq, L0_attn_bq, L0_attn_Wk, L0_attn_bk, L0_attn_Wv, L0_attn_bv, L0_attn_k_kernel, L0_attn_k_D, L0_attn_ssm_kernel, L0_attn_D, L0_attn_Wo, L0_attn_bo), axis=-1)
    x = _layernorm(x + _L0_ffn_ref(x, L0_ffn_W_fc, L0_ffn_W_proj), axis=-1)
    return x

_drawn_inputs = setup_inputs


def setup_inputs(seed=0):
    import zlib

    import numpy as np

    out = dict(_drawn_inputs(seed))
    spreads = {}
    factors = {'L0_attn_bq': 8.0,
     'L0_attn_bk': 8.0,
     'L0_attn_bv': 8.0,
     'L0_attn_k_kernel': 5.25,
     'L0_attn_k_D': 2.704,
     'L0_attn_ssm_kernel': 5.227}
    for name, (base, spread) in spreads.items():
        noise = np.random.default_rng([zlib.crc32(name.encode()), seed]).standard_normal(out[name].shape)
        drawn = base * np.exp(spread * noise) if base else spread * noise
        out[name] = jnp.asarray(drawn.astype(out[name].dtype))
    for name, factor in factors.items():
        out[name] = (out[name] * factor).astype(out[name].dtype)
    return out
```

```python
from contextlib import ExitStack

import concourse.bass as bass
from concourse import mybir

ALU = mybir.AluOpType
ACT = mybir.ActivationFunctionType
F32 = mybir.dt.float32
F16 = mybir.dt.float16
BF16 = mybir.dt.bfloat16
I32 = mybir.dt.int32
AX = mybir.AxisListType

P = 128
B, L, D, F = 16, 512, 256, 1024
NI = L // P
DT = D // P
FT = F // P
TOK = B * L
COL = NI * B
CH = 32
NC = D // CH
G = 8
GPC = CH // G
NG = D // G
HG = G // 2
HP = P // 2
ROWS = P + D * 2 * L
NU = 8
UP = TOK // NU
EPS = 1e-5
X1S = 2.0 ** 10

cW, cK1, cK2, cF, cP, cH, cLK, cLV, cBK, cBV, cL1 = range(11)
NST = 11


def spike_thresholds():
    import numpy as np
    one, beta = np.float32(1.0), np.float32(0.9)

    def spikes(bits):
        y = np.array(bits, np.int32).view(np.float32)
        mem, n = np.float32(0.0), 0
        for _ in range(5):
            reset = one if mem > one else np.float32(0.0)
            mem = np.float32(np.float32(np.float32(beta * mem) + y) - reset)
            n += bool(mem > one)
        return n

    found = []
    for n in range(1, 6):
        low, high = 0, int(np.array(4.0, np.float32).view(np.int32))
        while high - low > 1:
            mid = (low + high) // 2
            if spikes(mid) >= n:
                high = mid
            else:
                low = mid
        found.append(float(np.array(low, np.int32).view(np.float32)))
    return found


def build(nc, uT, u, wcat, wk_n, wv_n, bias, bo, k1, k2, kd1, kd2, woT, wf_n, wfT, wpT, out):
    theta = spike_thresholds()
    w16_dram = nc.dram_tensor("w16_dram", [P, NC, 2, DT * 3 * CH], F16, kind="Internal").ap()
    kpad_dram = nc.dram_tensor("kpad_dram", [2, 2, ROWS], F16, kind="Internal").ap()

    with ExitStack() as ctx:
        def sb(name, shape, dt):
            return ctx.enter_context(nc.sbuf_tensor(name, shape, dt))

        def sem(name):
            return ctx.enter_context(nc.semaphore(name))

        qy = sb("qy", [P, D * COL], F32)
        wf16 = sb("wf16", [P, 2, DT, F], F16)
        wp16 = sb("wp16", [P, 2, FT, D], F16)
        ident = sb("ident", [P, P], F32)
        st = sb("st", [P, 16], F32)
        gm = sb("gm", [P, 16], F32)
        um = sb("um", [P, NU + 2], F32)
        gu = sb("gu", [P, 1], F32)
        m2 = sb("m2", [P, 4], F32)
        s1 = sb("s1", [P, 6], F32)
        i1 = sb("i1", [P, 6], F32)
        s2 = sb("s2", [P, 3], F32)
        i2 = sb("i2", [P, 3], F32)
        srh = sb("srh", [P, 1], F32)
        tmp1 = sb("tmp1", [P, 16], F32)
        al = sb("al", [P, 8], F32)
        th = sb("th", [P, 8], F32)
        cell = sb("cell", [P, 2], F32)
        epsb = sb("epsb", [P, 1], F32)

        KB = 256
        arena = sb("arena", [P, 559 * KB // 4], F32)
        at = [0]

        def part(kb, shape, dt, pattern=None, **dims):
            a = arena[:, int(at[0]):int(at[0] + kb * KB)]
            at[0] += kb * KB
            if dt != F32:
                a = a.bitcast(dt)
            return a.rearrange(pattern, **dims) if pattern else a

        u16 = part(64, None, F16, "p (a t n) -> p a t n", a=2, t=DT)
        kv_at = at[0]
        k16 = part(16, None, F16, "p (r a n) -> p r a n", r=2, a=2)
        vbuf = part(16, None, F32, "p (r n) -> p r n", r=2)
        wcur = part(1.5, None, F16, "p (r a t n) -> p r a t n", r=2, a=2, t=DT)
        kv16 = part(4, None, F16, "p (r a n) -> p r a n", r=2, a=2)
        ktmp = part(2, None, F32, "p (r n) -> p r n", r=4)
        causal = part(0.25, None, F16)
        zeros = part(0.25, None, F16)
        bias_b = part(3, None, F32, "p (c s d) -> p c s d", c=NC, s=3)
        T = part(4 * 8, None, F16, "p (k c a n) -> p k c a n", k=4, c=HG, a=2)
        at[0] = 0
        wf_nat = part(8, None, F32, "p (t n) -> p t n", t=FT)
        wf_st = part(8, None, F32, "p (t n) -> p t n", t=DT)
        wp_st = part(8, None, F32, "p (t n) -> p t n", t=FT)
        junk = part(8, None, F32)
        w16 = part(6, None, F16, "p (c a x) -> p c a x", c=NC, a=2)
        at[0] = kv_at
        k_st = part(8, None, F32, "p (c t n) -> p c t n", c=2, t=DT)
        ksplit = part(8, None, F16, "p (c t a n) -> p c t a n", c=2, t=DT, a=2)
        w_st = part(6, None, F32, "p (c x) -> p c x", c=NC)
        wn_st = part(4, None, F32, "p (c t n) -> p c t n", c=2, t=DT)
        kd_st = part(0.25, None, F32)[:, 0:2 * DT].rearrange("p (c t) -> p c t", c=2)
        at[0] = 0
        wo = part(2, None, F32, "p (t n) -> p t n", t=DT)
        bo_b = part(1, None, F32)
        ub = part(8, None, F32, "p (r i n) -> p r i n", r=2, i=NI)
        yst = part(8, None, F32, "p (r i n) -> p r i n", r=2, i=NI)
        yT = part(4, None, F32, "p (t n) -> p t n", t=DT)
        rb = part(4, None, F32, "p (i n) -> p i n", i=NI)
        x1 = part(8, None, F32, "p (r i n) -> p r i n", r=2, i=NI)
        x16 = part(8, None, F16, "p (r a t n) -> p r a t n", r=2, a=2, t=DT)
        rl = part(8, None, F32, "p (r n) -> p r n", r=4)
        hh = part(8, None, F32, "p (r n) -> p r n", r=4)
        h16 = part(16, None, F16, "p (a f n) -> p a f n", a=2, f=FT)
        cnt = part(2, None, BF16)
        x2 = part(4, None, F32, "p (i n) -> p i n", i=NI)
        ob = part(8, None, F32, "p (r i n) -> p r i n", r=2, i=NI)
        bst = part(0.25, None, F32)[:, 0:48].rearrange("p (s i n) -> p s i n", s=2, i=NI)
        mv = part(0.25, None, F32)[:, 0:16].rearrange("p (s i n) -> p s i n", s=2, i=NI)
        sd = part(0.25, None, F32)[:, 0:8].rearrange("p (s i) -> p s i", s=2)
        rs = part(0.25, None, F32)[:, 0:8].rearrange("p (s i) -> p s i", s=2)
        nm = part(0.25, None, F32)[:, 0:8].rearrange("p (s i) -> p s i", s=2)

        ps = ctx.enter_context(nc.psum_tensor("ps", [P, 8, 512], F32))
        PA = ps[:, 0:4, :]
        PC1 = ps[:, 4:6, :]
        PC2 = ps[:, 6:8, :]
        PT = ps[:, 0:2, :]
        PW = ps[:, 2:4, :]
        PH = ps[:, 4:6, :]
        PD = ps[:, 6:8, :]

        ld_k, ld_w, ld_f, ld_b = sem("ld_k"), sem("ld_w"), sem("ld_f"), sem("ld_b")
        ld_u = [sem(f"ld_u{n}") for n in range(NU)]
        kpad_zero, kpad_hi, kpad_lo, kpad_out = sem("kpad_zero"), sem("kpad_hi"), sem("kpad_lo"), sem("kpad_out")
        id_zero, id_done = sem("id_zero"), sem("id_done")
        st_done, gm_done, um_done, gu_done = sem("st_done"), sem("gm_done"), sem("um_done"), sem("gu_done")
        squares = sem("squares")
        vlink = sem("vlink")
        scales1, scales2 = sem("scales1"), sem("scales2")
        w_hi, w_lo, f_hi, f_lo = sem("w_hi"), sem("w_lo"), sem("f_hi"), sem("f_lo")
        u_hi, u_lo = sem("u_hi"), sem("u_lo")
        t_in = [sem(f"t_in{n}") for n in range(4)]
        c1_masked, c2_masked = sem("c1_masked"), sem("c2_masked")
        c1_half, c2_half = sem("c1_half"), sem("c2_half")
        w16_out = sem("w16_out")
        ld_wcur = [sem(f"ld_wcur{r}") for r in range(2)]
        proj, proj_read = sem("proj"), sem("proj_read")
        ktmp_ready, k_hi, k_lo = sem("ktmp_ready"), sem("k_hi"), sem("k_lo")
        kv_ready, kv_hi, kv_lo = sem("kv_ready"), sem("kv_hi"), sem("kv_lo")
        y_ready = sem("y_ready")
        ld_wo = sem("ld_wo")
        ld_t = [sem(f"ld_t{n}") for n in range(2)]
        ub_ready, yst_ready = sem("ub_ready"), sem("yst_ready")
        y_turned, yT_ready, wo_done, r_ready = sem("y_turned"), sem("yT_ready"), sem("wo_done"), sem("r_ready")
        sd_ready, nm_ready, x1_ready = sem("sd_ready"), sem("nm_ready"), sem("x1_ready")
        sd2_ready, nm2_ready, ob_ready = sem("sd2_ready"), sem("nm2_ready"), sem("ob_ready")
        x_turned, x_hi, x_lo = sem("x_turned"), sem("x_hi"), sem("x_lo")
        up_done, rl_ready, hh_ready, h_hi, h_lo_v, h_lo_p = (sem("up_done"), sem("rl_ready"), sem("hh_ready"),
                                                            sem("h_hi"), sem("h_lo_v"), sem("h_lo_p"))
        down_done, stair, x2_ready = sem("down_done"), sem("stair"), sem("x2_ready")
        sum_ready, sum2_ready = sem("sum_ready"), sem("sum2_ready")
        moments = [sem(f"moments{n}") for n in range(2)]
        inverse = [sem(f"inverse{n}") for n in range(2)]
        stored = [sem(f"stored{n}") for n in range(2)]

        block = ctx.enter_context(nc.Block())
        GC = G * COL
        HC = HG * COL
        ust = qy[:, :].rearrange("p (t n) -> p t n", t=DT)

        def group_of(s):
            return (s % GPC) * GC

        PAIR = 2 * GPC

        def phase1(eng, step):
            with eng.Fori(0, NC // 2 - 1) as pair:
                for s in range(PAIR):
                    step(s, pair * PAIR, True)
            last = (NC // 2 - 1) * PAIR
            for s in range(PAIR):
                step(s, last, s < GPC)

        @block.sync
        def _(sp):
            for n in range(NU):
                sp.dma_start(ust[:, :, n * UP:(n + 1) * UP],
                             uT.rearrange("(t p) n -> p t n", p=P)[:, :, n * UP:(n + 1) * UP]).then_inc(ld_u[n], 16)
            sp.wait_ge(kpad_out, 96)

            def load_windows(conv, half, g):
                row = HG * 2 * L
                first = kpad_dram[conv, 0, P + (2 * g + half) * row:]
                sp.dma_start(T[:, 2 * conv + half].rearrange("p c a n -> p (c a n)"),
                             bass.AP(first.tensor, first.offset, [[ROWS - HP, 2], [-1, HP], [1, row]])
                             ).then_inc(t_in[2 * conv + half], 16)

            def load_w(chunk, r):
                sp.dma_start(wcur[:, r].rearrange("p a t x -> p (a t x)"),
                             w16_dram[:, bass.ds(chunk, 1)].rearrange("p c a x -> p (c a x)")
                             ).then_inc(ld_wcur[r], 16)

            for conv in range(2):
                for half in range(2):
                    load_windows(conv, half, 0)
            sp.wait_ge(w16_out, 16)
            load_w(0, 0)
            load_w(1, 1)
            for g in range(1, NG):
                chunk = g // GPC + 1
                if g % GPC == 0 and chunk < NC:
                    sp.wait_ge(proj, (chunk - 1) * B)
                    load_w(chunk, chunk % 2)
                for conv, used in ((0, c1_half), (1, c2_half)):
                    for half in range(2):
                        sp.wait_ge(used, 2 * g + half - 1)
                        load_windows(conv, half, g)

            sp.wait_ge(proj, NC * B)
            sp.dma_start(wo, woT.rearrange("(t p) n -> p t n", p=P)).then_inc(ld_wo, 16)
            sp.dma_start(bo_b[:, 0:D], bo.partition_broadcast(P)).then_inc(ld_wo, 16)

            def load_u(b, r):
                sp.dma_start(ub[:, r], u[bass.ds(b * NI, NI)].rearrange("i p n -> p i n")).then_inc(ld_t[r], 16)

            def store(b, r):
                sp.wait_ge(ob_ready, b + 1)
                sp.dma_start(out[bass.ds(b * NI, NI)].rearrange("i p n -> p i n"), ob[:, r]).then_inc(stored[r], 16)

            load_u(0, 0)
            load_u(1, 1)
            with sp.Fori(0, B // 2 - 1) as pair:
                for r in range(2):
                    b = pair * 2 + r
                    sp.wait_ge(r_ready, b + 1)
                    load_u(b + 2, r)
                    store(b, r)
            store(B - 2, 0)
            store(B - 1, 1)
            for r in range(2):
                sp.wait_ge(stored[r], 16 * (B // 2))

        @block.scalar
        def _(act):
            for c, (k, d) in enumerate(((k1, kd1), (k2, kd2))):
                act.dma_start(k_st[:, c], k.rearrange("(t p) n -> p t n", p=P)).then_inc(ld_k, 16)
                act.dma_start(kd_st[:, c], d.rearrange("(t p) -> p t", p=P),
                              allow_slow_non_contiguous=True).then_inc(ld_k, 16)
            act.dma_start(w_st, wcat).then_inc(ld_w, 16)
            act.dma_start(wn_st[:, 0], wk_n.rearrange("(t p) n -> p t n", p=P)).then_inc(ld_w, 16)
            act.dma_start(wn_st[:, 1], wv_n.rearrange("(t p) n -> p t n", p=P)).then_inc(ld_w, 16)
            act.dma_start(bias_b.rearrange("p c s d -> p (c s d)"), bias.partition_broadcast(P)).then_inc(ld_b, 16)
            act.dma_start(wf_nat, wf_n.rearrange("(t p) n -> p t n", p=P)).then_inc(ld_f, 16)
            act.dma_start(wf_st, wfT.rearrange("(t p) n -> p t n", p=P)).then_inc(ld_f, 16)
            act.dma_start(wp_st, wpT.rearrange("(t p) n -> p t n", p=P)).then_inc(ld_f, 16)
            act.wait_ge(ld_f, 48)
            for t in range(FT):
                nc.scalar.activation(junk[:, t * D:(t + 1) * D], wf_nat[:, t], ACT.Square,
                                     accum_out=tmp1[:, 8 + t:9 + t]).then_inc(squares, 1)
            act.wait_ge(scales1, 1)
            for c in range(2):
                nc.scalar.activation(ksplit[:, c, :, 0], k_st[:, c], ACT.Copy,
                                     scale=s1[:, cK1 + c:cK1 + c + 1]).then_inc(kpad_hi, 1)
            nc.scalar.activation(w16[:, :, 0], w_st, ACT.Copy, scale=s1[:, cW:cW + 1]).then_inc(w_hi, 1)
            nc.scalar.activation(wf16[:, 0], wf_st, ACT.Copy, scale=s1[:, cF:cF + 1]).then_inc(f_hi, 1)
            nc.scalar.activation(wp16[:, 0], wp_st, ACT.Copy, scale=s1[:, cP:cP + 1]).then_inc(f_hi, 1)
            act.wait_ge(kpad_lo, 2)
            act.wait_ge(kpad_hi, 2)
            act.wait_ge(kpad_zero, 1)
            for copy in range(2):
                for c in range(2):
                    act.dma_start(kpad_dram[c, copy, P:].rearrange("(t p n) -> p t n", p=P, t=DT),
                                  ksplit[:, c].rearrange("p t a n -> p t (a n)")).then_inc(kpad_out, 16)
                act.dma_start(kpad_dram[:, copy, 0:P], zeros[0:2, :]).then_inc(kpad_out, 16)
            act.wait_ge(w_lo, 1)
            act.wait_ge(w_hi, 1)
            act.dma_start(w16_dram, w16).then_inc(w16_out, 16)
            act.wait_ge(scales2, 1)
            act.wait_ge(w16_out, 16)
            act.wait_ge(f_lo, 2)
            act.wait_ge(squares, FT)
            for n in range(NU):
                nc.scalar.activation(u16[:, 0, :, n * UP:(n + 1) * UP], ust[:, :, n * UP:(n + 1) * UP], ACT.Copy,
                                     scale=s2[:, 0:1]).then_inc(u_hi, 1)

            def k_part(b, r, n, chunk):
                act.wait_ge(ktmp_ready, n + 1)
                dst = k16[:, r, 0].rearrange("p (d i b) -> p i d b", d=CH, i=NI)[:, :, :, b]
                nc.scalar.activation(dst, ktmp[:, b % 4].rearrange("p (i d) -> p i d", i=NI), ACT.Copy
                                     ).then_inc(k_hi, 1)

            def chunk0():
                act.wait_ge(kpad_out, 96)
                act.wait_ge(w_lo, 1)
                for b in range(B):
                    k_part(b, 0, b, 0)

            def step(s, base, more):
                g = base + s
                act.wait_ge(kv_ready, g + 1)
                if s >= 2 or not isinstance(base, int):
                    pass
                nc.scalar.activation(kv16[:, s % 2, 0], vbuf[:, s // GPC, group_of(s):group_of(s) + GC], ACT.Copy
                                     ).then_inc(kv_hi, 1)
                if more:
                    for b in range(4 * (s % GPC), 4 * (s % GPC) + 4):
                        k_part(b, (s // GPC + 1) % 2, (base // GPC + s // GPC + 1) * B + b
                               if isinstance(base, int) else base * (B // GPC) + (s // GPC + 1) * B + b, None)

            chunk0()
            phase1(act, step)

            nc.scalar.activation(sd[:, 0, 0:1], epsb[:, :], ACT.Sqrt)

            def y_turn(i):
                act.wait_ge(y_turned, i + 1)
                nc.scalar.activation(yT, PT, ACT.Copy).then_inc(yT_ready, 1)

            def norm(half, i, r):
                src, dst = (rb, x1[:, r]) if half == 0 else (x2, ob[:, r])
                act.wait_ge((r_ready, x2_ready)[half], i + 1)
                nc.scalar.activation(sd[:, half], mv[:, half, :, 1], ACT.Sqrt, bias=epsb[:, :]
                                     ).then_inc((sd_ready, sd2_ready)[half], 1)
                act.wait_ge((nm_ready, nm2_ready)[half], i + 1)
                for j in range(NI):
                    last = nc.scalar.activation(dst[:, j], src[:, j], ACT.Identity, bias=nm[:, half, j:j + 1],
                                                scale=rs[:, half, j:j + 1])
                last.then_inc((x1_ready, ob_ready)[half], 1)

            def x_turn(i, r):
                act.wait_ge(x_turned, i + 1)
                nc.scalar.activation(x16[:, r, 0], PT, ACT.Copy, scale=X1S).then_inc(x_hi, 1)

            def hidden_relu(i, f):
                act.wait_ge(up_done, i * FT + f + 1)
                if isinstance(i, int) and i == 0 and f < 4:
                    pass
                else:
                    act.wait_ge(hh_ready, i * FT + f - 3)
                nc.scalar.activation(rl[:, f % 4], PH[:, f % 2], ACT.Relu, scale=al[:, 4:5]).then_inc(rl_ready, 1)

            def hidden_hi(i, f):
                act.wait_ge(hh_ready, i * FT + f + 1)
                nc.scalar.activation(h16[:, 0, f], hh[:, f % 4], ACT.Copy).then_inc(h_hi, 1)

            def ahead(i, r):
                y_turn(i)

            def body(i, r, first, last):
                if not last:
                    y_turn(i + 1)
                if not first:
                    act.wait_ge(down_done, i * 2)
                for f in range(FT + 2):
                    if f < FT:
                        hidden_relu(i, f)
                    if f >= 2:
                        hidden_hi(i, f - 2)
                if not first:
                    act_store_wait(i, r)
                    norm(1, i - 1, 1 - r)
                if not last:
                    if not first:
                        pass
                    norm(0, i + 1, 1 - r)
                    x_turn(i + 1, 1 - r)

            def act_store_wait(i, r):
                if isinstance(i, int):
                    if i >= 3:
                        act.wait_ge(stored[1 - r], 16 * ((i - 1) // 2))
                elif r == 0:
                    act.wait_ge(stored[1], (i // 2 if False else stored_turn[0]) * 16)
                else:
                    act.wait_ge(stored[0], stored_turn[1] * 16)

            stored_turn = [0, 0]
            y_turn(0)
            norm(0, 0, 0)
            x_turn(0, 0)
            body(0, 0, True, False)
            body(1, 1, False, False)
            body(2, 0, False, False)
            with act.Fori(1, B // 2 - 1) as pair:
                stored_turn[1] = pair
                body(pair * 2 + 1, 1, False, False)
                stored_turn[0] = pair
                body(pair * 2 + 2, 0, False, False)
            body(B - 1, 1, False, True)
            act.wait_ge(stored[1], 16 * (B // 2 - 1))
            norm(1, B - 1, 1)

        @block.gpsimd
        def _(pool):
            nc.gpsimd.memset(ident[:, :], 0.0).then_inc(id_zero, 1)
            nc.gpsimd.memset(zeros, 0.0).then_inc(kpad_zero, 1)
            nc.gpsimd.memset(causal, 1.0).then_inc(id_zero, 1)
            nc.gpsimd.memset(epsb[:, :], EPS)
            pool.wait_ge(id_zero, 2)
            nc.gpsimd.affine_select(out=ident[:, :], in_=ident[:, :], compare_op=ALU.not_equal, fill=1.0,
                                    base=0, pattern=[[-1, P]], channel_multiplier=1).then_inc(id_done, 1)
            nc.gpsimd.affine_select(out=causal, in_=causal, compare_op=ALU.is_ge, fill=0.0,
                                    base=0, pattern=[[1, P]], channel_multiplier=-1).then_inc(id_done, 1)
            pool.wait_ge(st_done, 1)
            nc.gpsimd.partition_all_reduce(gm[:, 0:NST], st[:, 0:NST], P, bass.bass_isa.ReduceOp.max
                                           ).then_inc(gm_done, 1)
            pool.wait_ge(um_done, 1)
            nc.gpsimd.partition_all_reduce(gu[:, :], um[:, NU:NU + 1], P, bass.bass_isa.ReduceOp.max
                                           ).then_inc(gu_done, 1)

            def k_part(b, r, n):
                pool.wait_ge(k_hi, n + 1)
                dst = k16[:, r, :].rearrange("p a (d i b) -> p a i d b", d=CH, i=NI)[:, :, :, :, b]
                nc.gpsimd.tensor_tensor(dst[:, 1], ktmp[:, b % 4].rearrange("p (i d) -> p i d", i=NI), dst[:, 0],
                                        ALU.subtract).then_inc(k_lo, 1)

            for b in range(B):
                k_part(b, 0, b)

            def step(s, base, more):
                g = base + s
                pool.wait_ge(kv_hi, g + 1)
                nc.gpsimd.tensor_tensor(kv16[:, s % 2, 1], vbuf[:, s // GPC, group_of(s):group_of(s) + GC],
                                        kv16[:, s % 2, 0], ALU.subtract).then_inc(kv_lo, 1)
                if more:
                    for b in range(4 * (s % GPC), 4 * (s % GPC) + 4):
                        n = ((base // GPC + s // GPC + 1) * B + b if isinstance(base, int)
                             else base * (B // GPC) + (s // GPC + 1) * B + b)
                        k_part(b, (s // GPC + 1) % 2, n)

            with pool.Fori(0, NC // 2 - 1) as pair:
                for s in range(PAIR):
                    step(s, pair * PAIR, True)
            last = (NC // 2 - 1) * PAIR
            for s in range(PAIR):
                step(s, last, s < GPC)

            ysrc = qy[:, :].rearrange("p (d i b) -> p i d b", d=D, i=NI)

            def gather(i, r):
                if not isinstance(i, int) or i >= 2:
                    pool.wait_ge(y_turned, i - 1)
                nc.gpsimd.tensor_copy(yst[:, r], ysrc[:, :, :, bass.ds(i, 1)].rearrange("p i d b -> p i (d b)")
                                      ).then_inc(yst_ready, 1)

            def add_bo(i, r, nth):
                pool.wait_ge(ld_t[r], 16 * nth)
                nc.gpsimd.tensor_tensor(ub[:, r], ub[:, r],
                                        bo_b[:, 0:D].unsqueeze(1).to_broadcast([P, NI, D]), ALU.add
                                        ).then_inc(ub_ready, 1)

            def h_part(i, f):
                pool.wait_ge(h_hi, i * FT + f + 1)
                nc.gpsimd.tensor_tensor(h16[:, 1, f], hh[:, f % 4], h16[:, 0, f], ALU.subtract).then_inc(h_lo_p, 1)

            pool.wait_ge(y_ready, NG)
            pool.wait_ge(ld_wo, 32)
            gather(0, 0)
            add_bo(0, 0, 1)

            def body(i, r, nth, last):
                if not last:
                    gather(i + 1, 1 - r)
                    add_bo(i + 1, 1 - r, nth)
                for f in range(1, FT, 2):
                    h_part(i, f)

            body(0, 0, 1, False)
            with pool.Fori(0, B // 2 - 1) as pair:
                body(pair * 2 + 1, 1, pair + 2, False)
                body(pair * 2 + 2, 0, pair + 2, False)
            body(B - 1, 1, 0, True)

        @block.tensor
        def _(pe):
            def project(b, r, n, chunk_sem, piece=None):
                if piece is not None:
                    pe.wait_ge(u_lo, piece + 1)
                if not isinstance(n, int) or n >= 4:
                    pe.wait_ge(proj_read, n - 3)
                bank = PA[:, b % 4].rearrange("p (s x) -> p s x", s=4)[:, 0:3]
                for i in range(NI):
                    o = bank[:, :, i * CH:(i + 1) * CH]
                    tok = b * L + i * P
                    k = 0
                    for t in range(DT):
                        for x, w in ((0, 0), (0, 1), (1, 0)):
                            last = nc.tensor.matmul(o, u16[:, x, t, tok:tok + P],
                                                    wcur[:, r, w, t].rearrange("p (s x) -> p s x", s=3),
                                                    start=(k == 0), stop=(k == 3 * DT - 1))
                            k += 1
                last.then_inc(proj, 1)

            def convolve(conv, out, data, s, nth, done):
                for half in range(2):
                    pe.wait_ge((c1_masked, c2_masked)[conv], 2 * nth + half - 1)
                    for c in range(HG):
                        ch = half * HG + c
                        k = 0
                        for delta in range(NI):
                            cols = (NI - delta) * B
                            for tp, xp in ((0, 0), (0, 1), (1, 0)):
                                win = T[:, 2 * conv + half, c, tp]
                                last = nc.tensor.matmul(out[:, ch * COL + delta * B:(ch + 1) * COL],
                                                        win[:, delta * P:(delta + 1) * P],
                                                        data(xp, ch)[:, 0:cols],
                                                        start=(k == 0), stop=(k == 3 * NI - 1))
                                k += 1
                    last.then_inc(done, 1)

            pe.wait_ge(ld_wcur[0], 16)
            for b in range(B):
                project(b, 0, b, None, b // 2)

            def conv1(s, g, k_ready):
                pe.wait_ge(k_lo, k_ready)
                if not isinstance(g, int) or g >= 2:
                    pe.wait_ge(kv_ready, g - 1)
                convolve(0, PC1[:, s % 2], lambda a, ch: k16[:, s // GPC, a,
                                                             group_of(s) + ch * COL:group_of(s) + (ch + 1) * COL],
                         s, g + 1, c1_half)

            def conv2(s, g):
                pe.wait_ge(kv_lo, g + 1)
                if not isinstance(g, int) or g >= 2:
                    pe.wait_ge(y_ready, g - 1)
                convolve(1, PC2[:, s % 2], lambda a, ch: kv16[:, s % 2, a, ch * COL:(ch + 1) * COL],
                         s, g + 1, c2_half)

            def step(s, base, more, first=False):
                g = base + s
                tiles = base * (B // GPC) if not isinstance(base, int) else base // GPC * B
                conv1(s, g, tiles + (s // GPC + 1) * B)
                if more:
                    if s % GPC == 0:
                        pe.wait_ge(ld_wcur[(s // GPC + 1) % 2], (chunk_reg[0] + s // GPC + 1) * 16)
                    for b in range(4 * (s % GPC), 4 * (s % GPC) + 4):
                        project(b, (s // GPC + 1) % 2, tiles + (s // GPC + 1) * B + b, None)
                if not first:
                    conv2((s - 1) % PAIR, g - 1)

            chunk_reg = [0]
            for s in range(PAIR):
                step(s, 0, True, s == 0)
            with pe.Fori(1, NC // 2 - 1) as pair:
                chunk_reg[0] = pair
                for s in range(PAIR):
                    step(s, pair * PAIR, True)
            chunk_reg[0] = NC // 2 - 1
            for s in range(PAIR):
                step(s, NG - PAIR, s < GPC)
            conv2(PAIR - 1, NG - 1)

            def turn(src, done):
                for i in range(NI):
                    for t in range(DT):
                        last = nc.tensor.transpose(PT[:, t, i * P:(i + 1) * P], src[:, i, t * P:(t + 1) * P],
                                                   ident[:, :])
                last.then_inc(done, 1)

            def turn_y(i, r):
                pe.wait_ge(yst_ready, i + 1)
                if not isinstance(i, int) or i >= 1:
                    pe.wait_ge(x_lo, i)
                    pe.wait_ge(x_hi, i)
                turn(yst[:, r], y_turned)

            def project_out(i):
                pe.wait_ge(yT_ready, i + 1)
                if not isinstance(i, int) or i >= 1:
                    pe.wait_ge(r_ready, i)
                for j in range(NI):
                    for t in range(DT):
                        last = nc.tensor.matmul(PW[:, j // 2, (j % 2) * D:(j % 2 + 1) * D], yT[:, t, j * P:(j + 1) * P],
                                                wo[:, t], start=(t == 0), stop=(t == DT - 1))
                last.then_inc(wo_done, 1)

            def turn_x(i, r):
                pe.wait_ge(x1_ready, i + 1)
                turn(x1[:, r], x_turned)

            def up(i, r):
                pe.wait_ge(x_hi, i + 1)
                pe.wait_ge(x_lo, i + 1)
                for f in range(FT):
                    if not (isinstance(i, int) and i == 0 and f < 2):
                        pe.wait_ge(rl_ready, i * FT + f - 1)
                    k = 0
                    for t in range(DT):
                        for w, x in ((0, 0), (0, 1), (1, 0)):
                            last = nc.tensor.matmul(PH[:, f % 2], wf16[:, w, t, f * P:(f + 1) * P], x16[:, r, x, t],
                                                    start=(k == 0), stop=(k == 3 * DT - 1))
                            k += 1
                    last.then_inc(up_done, 1)

            def down(i, j):
                if j == 0:
                    pe.wait_ge(h_hi, (i + 1) * FT)
                    pe.wait_ge(h_lo_v, (i + 1) * (FT // 2))
                    pe.wait_ge(h_lo_p, (i + 1) * (FT // 2))
                    if not isinstance(i, int) or i >= 1:
                        pe.wait_ge(sum2_ready, i)
                k = 0
                for f in range(FT):
                    for h, w in ((0, 0), (0, 1), (1, 0)):
                        last = nc.tensor.matmul(PD[:, j // 2, (j % 2) * D:(j % 2 + 1) * D],
                                                h16[:, h, f, j * P:(j + 1) * P], wp16[:, w, f],
                                                start=(k == 0), stop=(k == 3 * FT - 1))
                        k += 1
                if j % 2:
                    last.then_inc(down_done, 1)

            def body(i, r, last):
                if not last:
                    turn_y(i + 1, 1 - r)
                up(i, r)
                if not last:
                    project_out(i + 1)
                for j in range(NI):
                    down(i, j)
                    if j == 2 and not last:
                        turn_x(i + 1, 1 - r)

            pe.wait_ge(id_done, 1)
            pe.wait_ge(ld_wo, 32)
            turn_y(0, 0)
            project_out(0)
            turn_x(0, 0)
            body(0, 0, False)
            with pe.Fori(0, B // 2 - 1) as pair:
                body(pair * 2 + 1, 1, False)
                body(pair * 2 + 2, 0, False)
            body(B - 1, 1, True)

        @block.vector
        def _(dve):
            links = [0]

            def link(ins):
                links[0] += 1
                ins.then_inc(vlink, 1)
                dve.wait_ge(vlink, links[0])

            def pow2(dst, inv, src, tmp):
                link(nc.vector.tensor_scalar(tmp, src, 1e-12, None, ALU.max))
                link(nc.vector.tensor_scalar(tmp.bitcast(I32), tmp.bitcast(I32), 0x7F800000, None, ALU.bitwise_and))
                link(nc.vector.tensor_scalar(dst.bitcast(I32), tmp.bitcast(I32), -1.0, float(268 << 23),
                                             ALU.mult, ALU.add))
                link(nc.vector.tensor_scalar(inv.bitcast(I32), dst.bitcast(I32), -1.0, float(254 << 23),
                                             ALU.mult, ALU.add))

            link(nc.vector.memset(st[:, :], 0.0))
            dve.wait_ge(ld_k, 64)
            for c in range(2):
                tap0 = k_st[:, c, :, 0:1].rearrange("p t o -> p (t o)")
                link(nc.vector.tensor_tensor(tap0, tap0, kd_st[:, c], ALU.add))

            def max_abs(dst, src, axis=AX.XY):
                link(nc.vector.tensor_reduce(dst, src, axis, ALU.max, apply_absolute_value=True))

            def max_of_row_sums(col, src, n):
                link(nc.vector.tensor_reduce(tmp1[:, 0:n], src, AX.X, ALU.add, apply_absolute_value=True))
                max_abs(st[:, col:col + 1], tmp1[:, 0:n], AX.X)

            for c in range(2):
                max_abs(st[:, cK1 + c:cK1 + c + 1], k_st[:, c])
            max_of_row_sums(cL1, k_st[:, 0], DT)
            dve.wait_ge(ld_w, 48)
            max_abs(st[:, cW:cW + 1], w_st)
            max_of_row_sums(cLK, wn_st[:, 0], DT)
            max_of_row_sums(cLV, wn_st[:, 1], DT)
            dve.wait_ge(ld_b, 16)
            for col, s in ((cBK, 0), (cBV, 1)):
                max_abs(st[:, col:col + 1], bias_b[:, :, s])
            dve.wait_ge(ld_f, 48)
            max_abs(st[:, cF:cF + 1], wf_st)
            max_abs(st[:, cP:cP + 1], wp_st)
            dve.wait_ge(squares, FT)
            max_abs(tmp1[:, 0:1], tmp1[:, 8:16], AX.X)
            nc.vector.tensor_scalar(st[:, cH:cH + 1], tmp1[:, 0:1], float(D) * 1.001, None, ALU.mult
                                    ).then_inc(st_done, 1)
            dve.wait_ge(gm_done, 1)
            pow2(s1[:, :], i1[:, :], gm[:, 0:6], tmp1[:, 0:6])
            b32 = srh[:, :].bitcast(I32)
            link(nc.vector.tensor_scalar(b32, s1[:, cH:cH + 1].bitcast(I32), 1, None, ALU.logical_shift_right))
            link(nc.vector.tensor_scalar(b32, b32, float(127 << 22), None, ALU.add))
            link(nc.vector.tensor_scalar(b32, b32, 0x7F800000, None, ALU.bitwise_and))
            link(nc.vector.tensor_scalar(al[:, 4:5], srh[:, :], i1[:, cF:cF + 1], 1.0 / X1S, ALU.mult, ALU.mult))
            link(nc.vector.tensor_scalar(tmp1[:, 0:1], srh[:, :], srh[:, :], s1[:, cP:cP + 1], ALU.mult, ALU.mult))
            for n, edge in enumerate(theta):
                last = nc.vector.tensor_scalar(th[:, n:n + 1], tmp1[:, 0:1], edge, None, ALU.mult)
            last.then_inc(scales1, 1)
            for c in range(2):
                dve.wait_ge(kpad_hi, c + 1)
                nc.vector.scalar_tensor_tensor(ksplit[:, c, :, 1], k_st[:, c], s1[:, cK1 + c:cK1 + c + 1],
                                               ksplit[:, c, :, 0], ALU.mult, ALU.subtract).then_inc(kpad_lo, 1)
            for n in range(NU):
                dve.wait_ge(ld_u[n], 16)
                max_abs(um[:, n:n + 1], ust[:, :, n * UP:(n + 1) * UP])
                if n == 0:
                    dve.wait_ge(w_hi, 1)
                    nc.vector.scalar_tensor_tensor(w16[:, :, 1], w_st, s1[:, cW:cW + 1], w16[:, :, 0],
                                                   ALU.mult, ALU.subtract).then_inc(w_lo, 1)
                if n == 2:
                    dve.wait_ge(f_hi, 1)
                    nc.vector.scalar_tensor_tensor(wf16[:, 1], wf_st, s1[:, cF:cF + 1], wf16[:, 0],
                                                   ALU.mult, ALU.subtract).then_inc(f_lo, 1)
                if n == 4:
                    dve.wait_ge(f_hi, 2)
                    nc.vector.scalar_tensor_tensor(wp16[:, 1], wp_st, s1[:, cP:cP + 1], wp16[:, 0],
                                                   ALU.mult, ALU.subtract).then_inc(f_lo, 1)
            nc.vector.tensor_reduce(um[:, NU:NU + 1], um[:, 0:NU], AX.X, ALU.max).then_inc(um_done, 1)
            dve.wait_ge(gu_done, 1)
            link(nc.vector.tensor_copy(m2[:, 0:1], gu[:, :]))
            link(nc.vector.tensor_scalar(tmp1[:, 0:1], gu[:, :], gm[:, cLV:cLV + 1], gm[:, cBV:cBV + 1],
                                         ALU.mult, ALU.add))
            link(nc.vector.tensor_scalar(m2[:, 1:2], gu[:, :], gm[:, cLK:cLK + 1], gm[:, cBK:cBK + 1],
                                         ALU.mult, ALU.add))
            link(nc.vector.tensor_scalar(m2[:, 2:3], m2[:, 1:2], gm[:, cL1:cL1 + 1], tmp1[:, 0:1],
                                         ALU.mult, ALU.mult))
            pow2(s2[:, :], i2[:, :], m2[:, 0:3], tmp1[:, 0:3])
            uw = al[:, 1:2]
            link(nc.vector.tensor_tensor(uw, i2[:, 0:1], i1[:, cW:cW + 1], ALU.mult))
            nc.vector.tensor_tensor(al[:, 0:1], uw, s2[:, 1:2], ALU.mult)
            nc.vector.tensor_scalar(al[:, 2:3], s2[:, 2:3], i2[:, 1:2], i1[:, cK1:cK1 + 1], ALU.mult, ALU.mult)
            nc.vector.tensor_tensor(al[:, 3:4], i2[:, 2:3], i1[:, cK2:cK2 + 1], ALU.mult)
            nc.vector.tensor_scalar(bias_b[:, :, 0], bias_b[:, :, 0], s2[:, 1:2], None, ALU.mult
                                    ).then_inc(scales2, 1)
            dve.wait_ge(scales2, 1)

            def split_u(n):
                dve.wait_ge(u_hi, n + 1)
                cols = slice(n * UP, (n + 1) * UP)
                nc.vector.scalar_tensor_tensor(u16[:, 1, :, cols], ust[:, :, cols], s2[:, 0:1], u16[:, 0, :, cols],
                                               ALU.mult, ALU.subtract).then_inc(u_lo, 1)

            qv = qy[:, :].rearrange("p (d i b) -> p i d b", d=D, i=NI)
            vv = vbuf.rearrange("p r (d i b) -> p r i d b", d=CH, i=NI)

            def read_projection(b, r, n, chunk):
                dve.wait_ge(proj, n + 1)
                if not isinstance(n, int) or n >= 4:
                    dve.wait_ge(k_lo, n - 3)
                for s, dst in ((0, ktmp[:, b % 4].rearrange("p (i d) -> p i d", i=NI)), (1, vv[:, r, :, :, b]),
                               (2, qv[:, :, bass.ds(chunk * CH, CH), b])):
                    bb = bias_b[:, bass.ds(chunk, 1), s].to_broadcast([P, NI, CH])
                    ins = nc.vector.scalar_tensor_tensor(
                        dst, PA[:, b % 4, s * P:(s + 1) * P].rearrange("p (i d) -> p i d", i=NI),
                        al[:, min(s, 1):min(s, 1) + 1], bb, ALU.mult, ALU.add)
                    if s == 0:
                        ins.then_inc(ktmp_ready, 1)
                    if s == 2:
                        ins.then_inc(proj_read, 1)

            split_u(0)
            split_u(1)
            dve.wait_ge(u_lo, 2)
            for n in range(2, NU):
                split_u(n)
                read_projection(2 * n - 4, 0, 2 * n - 4, 0)
                read_projection(2 * n - 3, 0, 2 * n - 3, 0)
            for b in range(2 * NU - 4, B):
                read_projection(b, 0, b, 0)

            def times_v(s, g, n):
                dve.wait_ge(c1_half, 2 * g + 2)
                dve.wait_ge(proj_read, n)
                v = vbuf[:, s // GPC, group_of(s):group_of(s) + GC]
                nc.vector.scalar_tensor_tensor(v, PC1[:, s % 2], al[:, 2:3], v, ALU.mult, ALU.mult
                                               ).then_inc(kv_ready, 1)

            def times_q(s, g):
                dve.wait_ge(c2_half, 2 * g + 2)
                q = qy[:, bass.ds(g * GC, GC)]
                nc.vector.scalar_tensor_tensor(q, PC2[:, s % 2], al[:, 3:4], q, ALU.mult, ALU.mult
                                               ).then_inc(y_ready, 1)

            def mask(conv, g):
                for half in range(2):
                    slot = 2 * conv + half
                    dve.wait_ge(t_in[slot], 16 * (g + 1))
                    tri = T[:, slot].rearrange("p c a n -> p (c a) n")[:, :, 0:P]
                    nc.vector.tensor_tensor(tri, tri, causal.unsqueeze(1).to_broadcast([P, 2 * HG, P]), ALU.mult
                                            ).then_inc((c1_masked, c2_masked)[conv], 1)

            def step(s, base, more, chunk, first=False):
                g = base + s
                tiles = base * (B // GPC) if not isinstance(base, int) else base // GPC * B
                mask(0, g)
                if not (first and s < 2):
                    times_q((s - 2) % PAIR, g - 2)
                times_v(s, g, tiles + (s // GPC + 1) * B)
                if more:
                    if s % GPC == 0 and not (first and s == 0):
                        dve.wait_ge(kv_lo, g)
                    for b in range(4 * (s % GPC), 4 * (s % GPC) + 4):
                        read_projection(b, (s // GPC + 1) % 2, tiles + (s // GPC + 1) * B + b,
                                        chunk + s // GPC + 1)
                if not (first and s == 0):
                    mask(1, g - 1)

            dve.wait_ge(id_done, 2)
            for s in range(PAIR):
                step(s, 0, True, 0, True)
            with dve.Fori(1, NC // 2 - 1) as pair:
                for s in range(PAIR):
                    step(s, pair * PAIR, True, pair * 2)
            for s in range(PAIR):
                step(s, NG - PAIR, s < GPC, NC - 2)
            mask(1, NG - 1)
            times_q(PAIR - 2, NG - 2)
            times_q(PAIR - 1, NG - 1)

            def norm_factors(half, i, src):
                dve.wait_ge((sum_ready, sum2_ready)[half], i + 1)
                for j in range(NI):
                    last = nc.vector.bn_stats(bst[:, half, j], src[:, j])
                last.then_inc(moments[half], 1)
                dve.wait_ge(moments[half], i + 1)
                nc.vector.memset(cell[:, half:half + 1], 0.0)
                for j in range(NI):
                    last = nc.vector.bn_aggr(mv[:, half, j], bst[:, half, j])
                last.then_inc((r_ready, x2_ready)[half], 1)

            def norm_inverse(half, i):
                dve.wait_ge((sd_ready, sd2_ready)[half], i + 1)
                nc.vector.reciprocal(rs[:, half], sd[:, half]).then_inc(inverse[half], 1)
                dve.wait_ge(inverse[half], i + 1)
                nc.vector.scalar_tensor_tensor(nm[:, half], mv[:, half, :, 0], -1.0, rs[:, half], ALU.mult, ALU.mult
                                               ).then_inc((nm_ready, nm2_ready)[half], 1)

            def first_sum(i, r):
                dve.wait_ge(wo_done, i + 1)
                dve.wait_ge(ub_ready, i + 1)
                if not isinstance(i, int) or i >= 1:
                    dve.wait_ge(x1_ready, i)
                nc.vector.tensor_tensor(rb.rearrange("p i n -> p (i n)"), PW.rearrange("p a n -> p (a n)"),
                                        ub[:, r].rearrange("p i n -> p (i n)"), ALU.add).then_inc(sum_ready, 1)
                norm_factors(0, i, rb)
                norm_inverse(0, i)

            def split_x(i, r):
                dve.wait_ge(x_hi, i + 1)
                nc.vector.scalar_tensor_tensor(x16[:, r, 1], PT, X1S, x16[:, r, 0], ALU.mult, ALU.subtract
                                               ).then_inc(x_lo, 1)

            def square(i, f):
                dve.wait_ge(rl_ready, i * FT + f + 1)
                if not (isinstance(i, int) and i == 0 and f < 4):
                    dve.wait_ge(h_lo_p if f % 2 else h_lo_v, i * (FT // 2) + f // 2 - 1)
                nc.vector.tensor_tensor(hh[:, f % 4], rl[:, f % 4], rl[:, f % 4], ALU.mult).then_inc(hh_ready, 1)

            def split_h(i, f):
                dve.wait_ge(h_hi, i * FT + f + 1)
                nc.vector.tensor_tensor(h16[:, 1, f], hh[:, f % 4], h16[:, 0, f], ALU.subtract).then_inc(h_lo_v, 1)

            def spikes(i, r, first):
                dve.wait_ge(down_done, 2 * i + 2)
                for n in range(len(theta)):
                    for half in range(2):
                        y, c = PD[:, half], cnt[:, half * 512:(half + 1) * 512]
                        k = 2 * n + half
                        if n == 0:
                            ins = nc.vector.tensor_scalar(c, y, th[:, 0:1], None, ALU.is_gt)
                        else:
                            dve.wait_ge(stair, i * 2 * len(theta) + k - 1)
                            ins = nc.vector.scalar_tensor_tensor(c, y, th[:, n:n + 1], c, ALU.is_gt, ALU.add)
                        ins.then_inc(stair, 1)
                dve.wait_ge(stair, (i + 1) * 2 * len(theta))
                if not first:
                    dve.wait_ge(ob_ready, i)
                nc.vector.scalar_tensor_tensor(x2.rearrange("p i n -> p (i n)"), cnt, 1.0 / len(theta),
                                               x1[:, r].rearrange("p i n -> p (i n)"), ALU.mult, ALU.add
                                               ).then_inc(sum2_ready, 1)
                norm_factors(1, i, x2)

            first_sum(0, 0)
            split_x(0, 0)

            def body(i, r, first, last):
                for f in range(FT + 2):
                    if f < FT:
                        square(i, f)
                    if f >= 2 and f % 2 == 0:
                        split_h(i, f - 2)
                if not first:
                    norm_inverse(1, i - 1)
                if not last:
                    first_sum(i + 1, 1 - r)
                    split_x(i + 1, 1 - r)
                spikes(i, r, first)

            body(0, 0, True, False)
            with dve.Fori(0, B // 2 - 1) as pair:
                body(pair * 2 + 1, 1, False, False)
                body(pair * 2 + 2, 0, False, False)
            body(B - 1, 1, False, True)
            norm_inverse(1, B - 1)


def kernel(**inputs):
    import numpy as np
    import concourse.bacc as bacc
    from concourse.bass_utils import run_bass_kernel_spmd

    f = {k[3:]: np.asarray(v) for k, v in inputs.items()}
    u = np.ascontiguousarray(f["attn_u"]).reshape(B * NI, P, D)
    wk, wv, wq = f["attn_Wk"], f["attn_Wv"], f["attn_Wq"]
    wcat = np.stack([w.T.reshape(D, NC, CH) for w in (wk, wv, wq)], axis=2)
    wcat = wcat.reshape(DT, P, NC, 3 * CH).transpose(1, 2, 0, 3).reshape(P, NC, DT * 3 * CH)
    bias = np.stack([f[n].reshape(NC, CH) for n in ("attn_bk", "attn_bv", "attn_bq")], axis=1).reshape(3 * D)
    arrays = {
        "uT": u.reshape(TOK, D).T, "u": u, "wcat": wcat, "wk_n": wk, "wv_n": wv, "bias": bias, "bo": f["attn_bo"],
        "k1": f["attn_k_kernel"], "k2": f["attn_ssm_kernel"], "kd1": f["attn_k_D"], "kd2": f["attn_D"],
        "woT": f["attn_Wo"].T, "wf_n": f["ffn_W_fc"], "wfT": f["ffn_W_fc"].T, "wpT": f["ffn_W_proj"].T,
    }
    nc = bacc.Bacc("TRN2", target_bir_lowering=False, num_devices=1, dynamic_dma_scratch_size=1024)
    ins, args = {}, []
    for name, a in arrays.items():
        ins[f"in_{name}"] = np.ascontiguousarray(a)
        args.append(nc.dram_tensor(f"in_{name}", a.shape, mybir.dt.from_np(a.dtype), kind="ExternalInput").ap())
    args.append(nc.dram_tensor("out", (B * NI, P, D), F32, kind="ExternalOutput").ap())
    build(nc, *args)
    r = run_bass_kernel_spmd(nc, [ins], core_ids=[0])
    return np.ascontiguousarray(r.results[0]["out"]).reshape(B, L, D)
```

```python
from contextlib import ExitStack

import concourse.bass as bass
from concourse import mybir

ALU = mybir.AluOpType
ACT = mybir.ActivationFunctionType
F32 = mybir.dt.float32
F16 = mybir.dt.float16
BF16 = mybir.dt.bfloat16
I32 = mybir.dt.int32
AX = mybir.AxisListType

P = 128
B, L, D, F = 16, 512, 256, 1024
NI = L // P
DT = D // P
FT = F // P
TOK = B * L
COL = NI * B
CH = 32
NC = D // CH
G = 8
GPC = CH // G
NG = D // G
HG = G // 2
HP = P // 2
ROWS = P + D * 2 * L
NU = 8
UP = TOK // NU
EPS = 1e-5
X1S = 2.0 ** 10

cW, cK1, cK2, cF, cP, cH, cLK, cLV, cBK, cBV, cL1 = range(11)
NST = 11


def spike_thresholds():
    import numpy as np
    one, beta = np.float32(1.0), np.float32(0.9)

    def spikes(bits):
        y = np.array(bits, np.int32).view(np.float32)
        mem, n = np.float32(0.0), 0
        for _ in range(5):
            reset = one if mem > one else np.float32(0.0)
            mem = np.float32(np.float32(np.float32(beta * mem) + y) - reset)
            n += bool(mem > one)
        return n

    found = []
    for n in range(1, 6):
        low, high = 0, int(np.array(4.0, np.float32).view(np.int32))
        while high - low > 1:
            mid = (low + high) // 2
            if spikes(mid) >= n:
                high = mid
            else:
                low = mid
        found.append(float(np.array(low, np.int32).view(np.float32)))
    return found


def build(nc, uT, u, wcat, wk_n, wv_n, bias, bo, k1, k2, kd1, kd2, woT, wf_n, wfT, wpT, out):
    theta = spike_thresholds()
    STAIRS = 2 * len(theta)
    w16_dram = nc.dram_tensor("w16_dram", [P, NC, 2, DT * 3 * CH], F16, kind="Internal").ap()
    kpad_dram = nc.dram_tensor("kpad_dram", [2, 2, ROWS], F16, kind="Internal").ap()

    with ExitStack() as ctx:
        def sb(name, shape, dt):
            return ctx.enter_context(nc.sbuf_tensor(name, shape, dt))

        def sem(name):
            return ctx.enter_context(nc.semaphore(name))

        qy = sb("qy", [P, D * COL], F32)
        ident = sb("ident", [P, P], F32)
        st = sb("st", [P, 16], F32)
        gm = sb("gm", [P, 16], F32)
        um = sb("um", [P, NU + 2], F32)
        gu = sb("gu", [P, 1], F32)
        m2 = sb("m2", [P, 4], F32)
        s1 = sb("s1", [P, 6], F32)
        i1 = sb("i1", [P, 6], F32)
        s2 = sb("s2", [P, 3], F32)
        i2 = sb("i2", [P, 3], F32)
        srh = sb("srh", [P, 1], F32)
        tmp1 = sb("tmp1", [P, 16], F32)
        al = sb("al", [P, 8], F32)
        th = sb("th", [P, 8], F32)
        cell = sb("cell", [P, 2], F32)
        eps = sb("eps", [P, NI], F32)
        half_neg = sb("half_neg", [P, NI], F32)

        KB = 256
        arena = sb("arena", [P, 628 * KB // 4], F32)
        at = [0]

        def part(kb, shape, dt, pattern=None, **dims):
            a = arena[:, int(at[0]):int(at[0] + kb * KB)]
            at[0] += kb * KB
            if dt != F32:
                a = a.bitcast(dt)
            return a.rearrange(pattern, **dims) if pattern else a

        u16 = part(64, None, F16, "p (a t n) -> p a t n", a=2, t=DT)
        kv_at = at[0]
        k16 = part(16, None, F16, "p (r a n) -> p r a n", r=2, a=2)
        vbuf = part(16, None, F32, "p (r n) -> p r n", r=2)
        wcur = part(1.5, None, F16, "p (r a t n) -> p r a t n", r=2, a=2, t=DT)
        kv16 = part(4, None, F16, "p (r a n) -> p r a n", r=2, a=2)
        ktmp = part(4, None, F32, "p (r n) -> p r n", r=2)
        causal = part(0.25, None, F16)
        zeros = part(0.25, None, F16)
        bias_b = part(3, None, F32, "p (c s d) -> p c s d", c=NC, s=3)
        T = part(6 * 8, None, F16, "p (k c a n) -> p k c a n", k=6, c=HG, a=2)
        at[0] = 0
        w16 = part(6, None, F16, "p (c a x) -> p c a x", c=NC, a=2)
        at[0] = kv_at
        k_st = part(8, None, F32, "p (c t n) -> p c t n", c=2, t=DT)
        ksplit = part(8, None, F16, "p (c t a n) -> p c t a n", c=2, t=DT, a=2)
        w_st = part(6, None, F32, "p (c x) -> p c x", c=NC)
        wn_st = part(4, None, F32, "p (c t n) -> p c t n", c=2, t=DT)
        kd_st = part(0.25, None, F32)[:, 0:2 * DT].rearrange("p (c t) -> p c t", c=2)
        at[0] = 0
        wf16 = part(8, None, F16, "p (a t n) -> p a t n", a=2, t=DT)
        wp16 = part(8, None, F16, "p (a t n) -> p a t n", a=2, t=FT)
        wo = part(2, None, F32, "p (t n) -> p t n", t=DT)
        bo_b = part(1, None, F32)
        stage_at = at[0]
        wf_nat = part(8, None, F32, "p (t n) -> p t n", t=FT)
        wf_st = part(8, None, F32, "p (t n) -> p t n", t=DT)
        wp_st = part(8, None, F32, "p (t n) -> p t n", t=FT)
        junk = part(8, None, F32)
        at[0] = stage_at
        hh = part(8, None, F32, "p (r n) -> p r n", r=4)
        h16 = part(16, None, F16, "p (a f n) -> p a f n", a=2, f=FT)
        yT = part(4, None, F32, "p (t n) -> p t n", t=DT)
        rb = part(4, None, F32, "p (i n) -> p i n", i=NI)
        ub = part(8, None, F32, "p (r i n) -> p r i n", r=2, i=NI)
        yst = part(8, None, F32, "p (r i n) -> p r i n", r=2, i=NI)
        x1 = part(8, None, F32, "p (r i n) -> p r i n", r=2, i=NI)
        x16 = part(8, None, F16, "p (r a t n) -> p r a t n", r=2, a=2, t=DT)
        rl = part(16, None, F32, "p (r n) -> p r n", r=FT)
        cnt = part(2, None, BF16)
        x2 = part(4, None, F32, "p (i n) -> p i n", i=NI)
        ob = part(8, None, F32, "p (r i n) -> p r i n", r=2, i=NI)
        bst = part(0.25, None, F32)[:, 0:48].rearrange("p (s i n) -> p s i n", s=2, i=NI)
        mv = part(0.25, None, F32)[:, 0:16].rearrange("p (s i n) -> p s i n", s=2, i=NI)
        ve = part(0.25, None, F32)[:, 0:8].rearrange("p (s i) -> p s i", s=2)
        rs = part(0.25, None, F32)[:, 0:8].rearrange("p (s i) -> p s i", s=2)
        nm = part(0.25, None, F32)[:, 0:8].rearrange("p (s i) -> p s i", s=2)

        ps = ctx.enter_context(nc.psum_tensor("ps", [P, 8, 512], F32))
        PA = ps[:, 0:4, :]
        PC1 = ps[:, 4:6, :]
        PC2 = ps[:, 6:8, :]
        PT = ps[:, 0:2, :]
        PW = ps[:, 2:4, :]
        PH = ps[:, 4:6, :]
        PD = ps[:, 6:8, :]

        ld_k, ld_w, ld_f, ld_b = sem("ld_k"), sem("ld_w"), sem("ld_f"), sem("ld_b")
        ld_u = [sem(f"ld_u{n}") for n in range(NU)]
        kpad_zero, kpad_hi, kpad_lo, kpad_out = sem("kpad_zero"), sem("kpad_hi"), sem("kpad_lo"), sem("kpad_out")
        id_zero, id_done = sem("id_zero"), sem("id_done")
        st_done, gm_done, um_done, gu_done = sem("st_done"), sem("gm_done"), sem("um_done"), sem("gu_done")
        squares = sem("squares")
        vlink = sem("vlink")
        scales1, scales2 = sem("scales1"), sem("scales2")
        w_hi, w_lo, f_hi, f_lo = sem("w_hi"), sem("w_lo"), sem("f_hi"), sem("f_lo")
        u_hi, u_lo = sem("u_hi"), sem("u_lo")
        t_in = [sem(f"t_in{n}") for n in range(6)]
        t_zero = sem("t_zero")
        c1_masked, c2_masked = sem("c1_masked"), sem("c2_masked")
        c1_copied, c2_copied = sem("c1_copied"), sem("c2_copied")
        c1_half, c2_half = sem("c1_half"), sem("c2_half")
        w16_out = sem("w16_out")
        ld_wcur = [sem(f"ld_wcur{r}") for r in range(2)]
        proj, proj_read = sem("proj"), sem("proj_read")
        ktmp_ready, k_hi, k_lo = sem("ktmp_ready"), sem("k_hi"), sem("k_lo")
        kv_ready, kv_hi, kv_lo = sem("kv_ready"), sem("kv_hi"), sem("kv_lo")
        y_ready = sem("y_ready")
        ld_wo = sem("ld_wo")
        ld_t = [sem(f"ld_t{n}") for n in range(2)]
        ub_ready, yst_ready = sem("ub_ready"), sem("yst_ready")
        y_turned, yT_ready, wo_done, r_ready = sem("y_turned"), sem("yT_ready"), sem("wo_done"), sem("r_ready")
        ve_ready = [sem(f"ve_ready{n}") for n in range(2)]
        rs_ready, nm_ready, x1_ready = sem("rs_ready"), sem("nm_ready"), sem("x1_ready")
        rs2_ready, nm2_ready, ob_ready = sem("rs2_ready"), sem("nm2_ready"), sem("ob_ready")
        x_turned, x_hi, x_lo = sem("x_turned"), sem("x_hi"), sem("x_lo")
        up_done, rl_ready, hh_ready = sem("up_done"), sem("rl_ready"), sem("hh_ready")
        h_hi, h_lo = sem("h_hi"), sem("h_lo")
        down_done, stair, x2_ready = sem("down_done"), sem("stair"), sem("x2_ready")
        sum_ready, sum2_ready = sem("sum_ready"), sem("sum2_ready")
        moments = [sem(f"moments{n}") for n in range(2)]
        st2_done, gm2_done, scales3 = sem("st2_done"), sem("gm2_done"), sem("scales3")
        stored = [sem(f"stored{n}") for n in range(2)]

        block = ctx.enter_context(nc.Block())
        GC = G * COL
        HC = HG * COL
        ust = qy[:, :].rearrange("p (t n) -> p t n", t=DT)
        ysrc = qy[:, :].rearrange("p (d i b) -> p i d b", d=D, i=NI)

        def quarter_of(a, quarter):
            return a.rearrange("p (d i b) -> p b i d", d=CH, i=NI)[:, 4 * quarter:4 * quarter + 4]

        def dense(a):
            return a.rearrange("p (b i d) -> p b i d", b=4, i=NI)

        def group_of(s):
            return (s % GPC) * GC

        def shifted(slot):
            t = T[:, slot].rearrange("p c a n -> p (c a) n")
            return t[HP:P, :, HP:L], t[0:HP, :, 0:L - HP]

        PAIR = 2 * GPC

        def phase1(eng, step):
            with eng.Fori(0, NC // 2 - 1) as pair:
                for s in range(PAIR):
                    step(s, pair * PAIR, True)
            last = (NC // 2 - 1) * PAIR
            for s in range(PAIR):
                step(s, last, s < GPC)

        @block.sync
        def _(sp):
            for c, k in enumerate((k1, k2)):
                sp.dma_start(k_st[:, c], k.rearrange("(t p) n -> p t n", p=P)).then_inc(ld_k, 16)
            sp.dma_start(w_st, wcat).then_inc(ld_w, 16)
            for c, w in enumerate((wk_n, wv_n)):
                sp.dma_start(wn_st[:, c], w.rearrange("(t p) n -> p t n", p=P)).then_inc(ld_w, 16)
            for n in range(NU):
                sp.dma_start(ust[:, :, n * UP:(n + 1) * UP],
                             uT.rearrange("(t p) n -> p t n", p=P)[:, :, n * UP:(n + 1) * UP]).then_inc(ld_u[n], 16)
            sp.wait_ge(kpad_out, 96)

            def load_windows(conv, half, g):
                row = HG * 2 * L
                first = kpad_dram[conv, 0, P + (2 * g + half) * row:]
                slot = 4 + half if conv else g % 2 * 2 + half
                sp.dma_start(T[0:HP, slot].rearrange("p c a n -> p (c a n)"),
                             bass.AP(first.tensor, first.offset, [[ROWS - HP // 2, 2], [-1, HP // 2], [1, row]])
                             ).then_inc(t_in[slot], 16)

            def load_w(chunk, r):
                sp.dma_start(wcur[:, r].rearrange("p a t x -> p (a t x)"),
                             w16_dram[:, bass.ds(chunk, 1)].rearrange("p c a x -> p (c a x)")
                             ).then_inc(ld_wcur[r], 16)

            for conv, g in ((0, 0), (0, 1), (1, 0)):
                for half in range(2):
                    load_windows(conv, half, g)
            sp.wait_ge(w16_out, 16)
            load_w(0, 0)
            load_w(1, 1)
            for s in range(NG):
                chunk = s // GPC + 2
                if s % GPC == 0 and chunk < NC:
                    sp.wait_ge(proj, GPC * (chunk - 1))
                    load_w(chunk, chunk % 2)
                if s + 2 < NG:
                    for half in range(2):
                        sp.wait_ge(c1_half, 2 * s + half + 1)
                        load_windows(0, half, s + 2)
                if s:
                    for half in range(2):
                        sp.wait_ge(c2_half, 2 * s + half - 1)
                        load_windows(1, half, s)
                if s == NG - GPC - 1:
                    sp.wait_ge(proj, GPC * NC)
                    sp.dma_start(wf_nat, wf_n.rearrange("(t p) n -> p t n", p=P)).then_inc(ld_f, 16)
                if s == NG - GPC:
                    sp.dma_start(wf_st, wfT.rearrange("(t p) n -> p t n", p=P)).then_inc(ld_f, 16)
                if s == NG - GPC + 1:
                    sp.dma_start(wp_st, wpT.rearrange("(t p) n -> p t n", p=P)).then_inc(ld_f, 16)
            sp.dma_start(wo, woT.rearrange("(t p) n -> p t n", p=P)).then_inc(ld_wo, 16)
            sp.dma_start(bo_b[:, 0:D], bo.partition_broadcast(P)).then_inc(ld_wo, 16)

            def load_u(b, r):
                sp.dma_start(ub[:, r], u[bass.ds(b * NI, NI)].rearrange("i p n -> p i n")).then_inc(ld_t[r], 16)

            def store(b, r):
                sp.wait_ge(ob_ready, b + 1)
                sp.dma_start(out[bass.ds(b * NI, NI)].rearrange("i p n -> p i n"), ob[:, r]).then_inc(stored[r], 16)

            load_u(0, 0)
            load_u(1, 1)
            with sp.Fori(0, B // 2 - 1) as pair:
                for r in range(2):
                    b = pair * 2 + r
                    sp.wait_ge(r_ready, b + 1)
                    load_u(b + 2, r)
                    store(b, r)
            store(B - 2, 0)
            store(B - 1, 1)
            for r in range(2):
                sp.wait_ge(stored[r], 16 * (B // 2))

        @block.scalar
        def _(act):
            for c, d in enumerate((kd1, kd2)):
                act.dma_start(kd_st[:, c], d.rearrange("(t p) -> p t", p=P),
                              allow_slow_non_contiguous=True).then_inc(ld_k, 16)
            act.dma_start(bias_b.rearrange("p c s d -> p (c s d)"), bias.partition_broadcast(P)).then_inc(ld_b, 16)
            act.wait_ge(scales1, 1)
            for c in range(2):
                nc.scalar.activation(ksplit[:, c, :, 0], k_st[:, c], ACT.Copy,
                                     scale=s1[:, cK1 + c:cK1 + c + 1]).then_inc(kpad_hi, 1)
            nc.scalar.activation(w16[:, :, 0], w_st, ACT.Copy, scale=s1[:, cW:cW + 1]).then_inc(w_hi, 1)
            act.wait_ge(kpad_lo, 2)
            act.wait_ge(kpad_hi, 2)
            act.wait_ge(kpad_zero, 1)
            for copy in range(2):
                for c in range(2):
                    act.dma_start(kpad_dram[c, copy, P:].rearrange("(t p n) -> p t n", p=P, t=DT),
                                  ksplit[:, c].rearrange("p t a n -> p t (a n)")).then_inc(kpad_out, 16)
                act.dma_start(kpad_dram[:, copy, 0:P], zeros[0:2, :]).then_inc(kpad_out, 16)
            act.wait_ge(w_lo, 1)
            act.wait_ge(w_hi, 1)
            act.dma_start(w16_dram, w16).then_inc(w16_out, 16)
            act.wait_ge(scales2, 1)
            act.wait_ge(w16_out, 16)
            for n in range(NU):
                nc.scalar.activation(u16[:, 0, :, n * UP:(n + 1) * UP], ust[:, :, n * UP:(n + 1) * UP], ACT.Copy,
                                     scale=s2[:, 0:1]).then_inc(u_hi, 1)

            def k_part(quarter, r, n):
                act.wait_ge(ktmp_ready, n + 1)
                nc.scalar.activation(quarter_of(k16[:, r, 0], quarter), dense(ktmp[:, quarter % 2]), ACT.Copy
                                     ).then_inc(k_hi, 1)

            def copy_windows(s, g, half):
                act.wait_ge(c1_masked, 2 * g + half + 1)
                nc.scalar.activation(*shifted(s % 2 * 2 + half), ACT.Copy).then_inc(c1_copied, 1)

            def step(s, base, more):
                if not (isinstance(base, int) and base + s == NG - 1):
                    for half in range(2):
                        copy_windows(s + 1, base + s + 1, half)
                if more:
                    k_part(s % GPC, (s // GPC + 1) % 2, base + s + GPC)
                act.wait_ge(kv_ready, base + s + 1)
                nc.scalar.activation(kv16[:, s % 2, 0], vbuf[:, s // GPC, group_of(s):group_of(s) + GC], ACT.Copy
                                     ).then_inc(kv_hi, 1)

            act.wait_ge(kpad_out, 96)
            act.wait_ge(w_lo, 1)
            copy_windows(0, 0, 0)
            copy_windows(0, 0, 1)
            for quarter in range(GPC):
                k_part(quarter, 0, quarter)
            with act.Fori(0, NC // 2 - 1) as pair:
                for s in range(PAIR):
                    step(s, pair * PAIR, True)
            for s in range(PAIR):
                step(s, NG - PAIR, s < GPC)
                if s == PAIR - 2:
                    act.wait_ge(ld_f, 48)
                    for t in range(FT):
                        nc.scalar.activation(junk[:, t * D:(t + 1) * D], wf_nat[:, t], ACT.Square,
                                             accum_out=tmp1[:, 8 + t:9 + t]).then_inc(squares, 1)
            act.wait_ge(scales3, 1)
            nc.scalar.activation(wf16[:, 0], wf_st, ACT.Copy, scale=s1[:, cF:cF + 1]).then_inc(f_hi, 1)
            nc.scalar.activation(wp16[:, 0], wp_st, ACT.Copy, scale=s1[:, cP:cP + 1]).then_inc(f_hi, 1)


            def y_turn(i):
                act.wait_ge(y_turned, i + 1)
                nc.scalar.activation(yT, PT, ACT.Copy).then_inc(yT_ready, 1)

            def norm(half, i, r):
                src, dst = (rb, x1[:, r]) if half == 0 else (x2, ob[:, r])
                act.wait_ge((nm_ready, nm2_ready)[half], i + 1)
                for j in range(NI):
                    last = nc.scalar.activation(dst[:, j], src[:, j], ACT.Identity, bias=nm[:, half, j:j + 1],
                                                scale=rs[:, half, j:j + 1])
                last.then_inc((x1_ready, ob_ready)[half], 1)

            def x_turn(i, r):
                act.wait_ge(x_turned, i + 1)
                nc.scalar.activation(x16[:, r, 0], PT, ACT.Copy, scale=X1S).then_inc(x_hi, 1)

            def hidden_relu(i, f):
                act.wait_ge(up_done, i * FT + f + 1)
                if not isinstance(i, int) or i >= 1:
                    act.wait_ge(hh_ready, i * FT + f - FT + 1)
                nc.scalar.activation(rl[:, f], PH[:, f % 2], ACT.Relu, scale=al[:, 4:5]).then_inc(rl_ready, 1)

            def hidden_hi(i, f):
                act.wait_ge(hh_ready, i * FT + f + 1)
                nc.scalar.activation(h16[:, 0, f], hh[:, f % 4], ACT.Copy).then_inc(h_hi, 1)

            def body(i, r, first, last):
                if not last:
                    y_turn(i + 1)
                if not first:
                    act.wait_ge(down_done, i * 2)
                for f in range(FT + 4):
                    if f < FT:
                        hidden_relu(i, f)
                    if f >= 4:
                        hidden_hi(i, f - 4)
                if not first:
                    act_store_wait(i, r)
                    norm(1, i - 1, 1 - r)
                if not last:
                    norm(0, i + 1, 1 - r)
                    x_turn(i + 1, 1 - r)

            def act_store_wait(i, r):
                if isinstance(i, int):
                    if i >= 3:
                        act.wait_ge(stored[1 - r], 16 * ((i - 1) // 2))
                elif r == 0:
                    act.wait_ge(stored[1], (i // 2 if False else stored_turn[0]) * 16)
                else:
                    act.wait_ge(stored[0], stored_turn[1] * 16)

            stored_turn = [0, 0]
            act.wait_ge(y_ready, NG)
            nc.scalar.activation(yst[:, 0], ysrc[:, :, :, 0], ACT.Copy).then_inc(yst_ready, 1)
            y_turn(0)
            norm(0, 0, 0)
            x_turn(0, 0)
            body(0, 0, True, False)
            body(1, 1, False, False)
            body(2, 0, False, False)
            with act.Fori(1, B // 2 - 1) as pair:
                stored_turn[1] = pair
                body(pair * 2 + 1, 1, False, False)
                stored_turn[0] = pair
                body(pair * 2 + 2, 0, False, False)
            body(B - 1, 1, False, True)
            act.wait_ge(stored[1], 16 * (B // 2 - 1))
            norm(1, B - 1, 1)

        @block.gpsimd
        def _(pool):
            nc.gpsimd.memset(ident[:, :], 0.0).then_inc(id_zero, 1)
            nc.gpsimd.memset(zeros, 0.0).then_inc(kpad_zero, 1)
            nc.gpsimd.memset(causal, 1.0).then_inc(id_zero, 1)
            nc.gpsimd.memset(half_neg[:, :], -0.5).then_inc(id_zero, 1)
            nc.gpsimd.memset(eps[:, :], EPS).then_inc(id_zero, 1)
            pool.wait_ge(id_zero, 4)
            nc.gpsimd.affine_select(out=ident[:, :], in_=ident[:, :], compare_op=ALU.not_equal, fill=1.0,
                                    base=0, pattern=[[-1, P]], channel_multiplier=1).then_inc(id_done, 1)
            nc.gpsimd.affine_select(out=causal, in_=causal, compare_op=ALU.is_ge, fill=0.0,
                                    base=0, pattern=[[1, P]], channel_multiplier=-1).then_inc(id_done, 1)
            pool.wait_ge(st_done, 1)
            nc.gpsimd.partition_all_reduce(gm[:, 0:NST], st[:, 0:NST], P, bass.bass_isa.ReduceOp.max
                                           ).then_inc(gm_done, 1)
            pool.wait_ge(um_done, 1)
            nc.gpsimd.partition_all_reduce(gu[:, :], um[:, NU:NU + 1], P, bass.bass_isa.ReduceOp.max
                                           ).then_inc(gu_done, 1)

            def k_part(quarter, r, n):
                pool.wait_ge(k_hi, n + 1)
                nc.gpsimd.tensor_tensor(quarter_of(k16[:, r, 1], quarter), dense(ktmp[:, quarter % 2]),
                                        quarter_of(k16[:, r, 0], quarter), ALU.subtract).then_inc(k_lo, 1)

            def step(s, base, more):
                if more:
                    k_part(s % GPC, (s // GPC + 1) % 2, base + s + GPC)
                pool.wait_ge(kv_hi, base + s + 1)
                nc.gpsimd.tensor_tensor(kv16[:, s % 2, 1], vbuf[:, s // GPC, group_of(s):group_of(s) + GC],
                                        kv16[:, s % 2, 0], ALU.subtract).then_inc(kv_lo, 1)

            for quarter in range(GPC):
                k_part(quarter, 0, quarter)
            phase1(pool, step)
            pool.wait_ge(st2_done, 1)
            nc.gpsimd.partition_all_reduce(gm[:, cF:cF + 3], st[:, cF:cF + 3], P, bass.bass_isa.ReduceOp.max
                                           ).then_inc(gm2_done, 1)

            def gather(i, r):
                if not isinstance(i, int):
                    pool.wait_ge(y_turned, i - 1)
                nc.gpsimd.tensor_copy(yst[:, r], ysrc[:, :, :, bass.ds(i, 1)].rearrange("p i d b -> p i (d b)")
                                      ).then_inc(yst_ready, 1)

            def add_bo(i, r, nth):
                pool.wait_ge(ld_t[r], 16 * nth)
                nc.gpsimd.tensor_tensor(ub[:, r], ub[:, r],
                                        bo_b[:, 0:D].unsqueeze(1).to_broadcast([P, NI, D]), ALU.add
                                        ).then_inc(ub_ready, 1)

            def h_part(i, f):
                pool.wait_ge(h_hi, i * FT + f + 1)
                nc.gpsimd.tensor_tensor(h16[:, 1, f], hh[:, f % 4], h16[:, 0, f], ALU.subtract).then_inc(h_lo, 1)

            def root(half, i):
                pool.wait_ge((r_ready, x2_ready)[half], i + 1)
                nc.gpsimd.tensor_tensor(ve[:, half], mv[:, half, :, 1], eps[:, :], ALU.add
                                        ).then_inc(ve_ready[half], 1)
                pool.wait_ge(ve_ready[half], i + 1)
                nc.gpsimd.tensor_tensor(rs[:, half], ve[:, half], half_neg[:, :], ALU.pow
                                        ).then_inc((rs_ready, rs2_ready)[half], 1)

            pool.wait_ge(ld_wo, 32)
            add_bo(0, 0, 1)
            pool.wait_ge(y_ready, NG)
            pool.wait_ge(yst_ready, 1)
            gather(1, 1)
            root(0, 0)
            add_bo(1, 1, 1)

            def body(i, r, nth, left):
                for f in range(FT):
                    h_part(i, f)
                if left:
                    root(0, i + 1)
                if left > 1:
                    gather(i + 2, r)
                    add_bo(i + 2, r, nth)
                root(1, i)

            with pool.Fori(0, B // 2 - 1) as pair:
                body(pair * 2, 0, pair + 2, 2)
                body(pair * 2 + 1, 1, pair + 2, 2)
            body(B - 2, 0, 0, 1)
            body(B - 1, 1, 0, 0)

        @block.tensor
        def _(pe):
            def project(quarter, r, n, pieces=None):
                if pieces is not None:
                    pe.wait_ge(u_lo, pieces)
                if not isinstance(n, int) or n >= 1:
                    pe.wait_ge(proj_read, n)
                for b in range(4 * quarter, 4 * quarter + 4):
                    for i in range(NI):
                        o = PA[:, b % 4, i * P:i * P + 3 * CH]
                        tok = b * L + i * P
                        k = 0
                        for t in range(DT):
                            for x, w in ((0, 0), (0, 1), (1, 0)):
                                last = nc.tensor.matmul(o, u16[:, x, t, tok:tok + P],
                                                        wcur[:, r, w, t],
                                                        start=(k == 0), stop=(k == 3 * DT - 1))
                                k += 1
                last.then_inc(proj, 1)

            def convolve(conv, out, data, s, nth, done):
                for half in range(2):
                    pe.wait_ge((c1_copied, c2_copied)[conv], 2 * nth + half - 1)
                    for c in range(HG):
                        ch = half * HG + c
                        k = 0
                        for delta in range(NI):
                            cols = (NI - delta) * B
                            for tp, xp in ((0, 0), (0, 1), (1, 0)):
                                win = T[:, 4 + half if conv else s % 2 * 2 + half, c, tp]
                                last = nc.tensor.matmul(out[:, ch * COL + delta * B:(ch + 1) * COL],
                                                        win[:, delta * P:(delta + 1) * P],
                                                        data(xp, ch)[:, 0:cols],
                                                        start=(k == 0), stop=(k == 3 * NI - 1))
                                k += 1
                    last.then_inc(done, 1)

            pe.wait_ge(ld_wcur[0], 16)
            for quarter in range(GPC):
                project(quarter, 0, quarter, (quarter + 1) * NU // GPC)

            def conv1(s, g, k_ready):
                pe.wait_ge(k_lo, k_ready)
                if not isinstance(g, int) or g >= 2:
                    pe.wait_ge(kv_ready, g - 1)
                convolve(0, PC1[:, s % 2], lambda a, ch: k16[:, s // GPC, a,
                                                             group_of(s) + ch * COL:group_of(s) + (ch + 1) * COL],
                         s, g + 1, c1_half)

            def conv2(s, g):
                pe.wait_ge(kv_lo, g + 1)
                if not isinstance(g, int) or g >= 2:
                    pe.wait_ge(y_ready, g - 1)
                convolve(1, PC2[:, s % 2], lambda a, ch: kv16[:, s % 2, a, ch * COL:(ch + 1) * COL],
                         s, g + 1, c2_half)

            def step(s, base, more, first=False):
                g = base + s
                if more:
                    if s % GPC == 0:
                        pe.wait_ge(ld_wcur[(s // GPC + 1) % 2], (chunk_reg[0] + s // GPC + 1) * 16)
                    project(s % GPC, (s // GPC + 1) % 2, g + GPC)
                conv1(s, g, base + (s // GPC + 1) * GPC)
                if not first:
                    conv2((s - 1) % PAIR, g - 1)

            chunk_reg = [0]
            for s in range(PAIR):
                step(s, 0, True, s == 0)
            with pe.Fori(1, NC // 2 - 1) as pair:
                chunk_reg[0] = pair
                for s in range(PAIR):
                    step(s, pair * PAIR, True)
            chunk_reg[0] = NC // 2 - 1
            for s in range(PAIR):
                step(s, NG - PAIR, s < GPC)
            conv2(PAIR - 1, NG - 1)

            def turn(src, done):
                for i in range(NI):
                    for t in range(DT):
                        last = nc.tensor.transpose(PT[:, t, i * P:(i + 1) * P], src[:, i, t * P:(t + 1) * P],
                                                   ident[:, :])
                last.then_inc(done, 1)

            def turn_y(i, r):
                pe.wait_ge(yst_ready, i + 1)
                if not isinstance(i, int) or i >= 1:
                    pe.wait_ge(x_lo, i)
                    pe.wait_ge(x_hi, i)
                turn(yst[:, r], y_turned)

            def project_out(i):
                pe.wait_ge(yT_ready, i + 1)
                if not isinstance(i, int) or i >= 1:
                    pe.wait_ge(r_ready, i)
                for j in range(NI):
                    for t in range(DT):
                        last = nc.tensor.matmul(PW[:, j // 2, (j % 2) * D:(j % 2 + 1) * D], yT[:, t, j * P:(j + 1) * P],
                                                wo[:, t], start=(t == 0), stop=(t == DT - 1))
                last.then_inc(wo_done, 1)

            def turn_x(i, r):
                pe.wait_ge(x1_ready, i + 1)
                turn(x1[:, r], x_turned)

            def up(i, r):
                pe.wait_ge(x_hi, i + 1)
                pe.wait_ge(x_lo, i + 1)
                for f in range(FT):
                    if not (isinstance(i, int) and i == 0 and f < 2):
                        pe.wait_ge(rl_ready, i * FT + f - 1)
                    k = 0
                    for t in range(DT):
                        for w, x in ((0, 0), (0, 1), (1, 0)):
                            last = nc.tensor.matmul(PH[:, f % 2], wf16[:, w, t, f * P:(f + 1) * P], x16[:, r, x, t],
                                                    start=(k == 0), stop=(k == 3 * DT - 1))
                            k += 1
                    last.then_inc(up_done, 1)

            def down_part(i, j, f, h, w, first, last):
                return nc.tensor.matmul(PD[:, j // 2, (j % 2) * D:(j % 2 + 1) * D],
                                        h16[:, h, f, j * P:(j + 1) * P], wp16[:, w, f], start=first, stop=last)

            def down_first(i):
                if not isinstance(i, int) or i >= 1:
                    pe.wait_ge(stair, i * STAIRS)
                for f in range(FT):
                    pe.wait_ge(h_hi, i * FT + f + 1)
                    for j in (0, 2):
                        for w in range(2):
                            down_part(i, j, f, 0, w, f == 0 and w == 0, False)
                for f in range(FT):
                    pe.wait_ge(h_lo, i * FT + f + 1)
                    for j in (0, 2):
                        down_part(i, j, f, 1, 0, False, f == FT - 1)

            def down(i, j):
                for f in range(FT):
                    for h, w in ((0, 0), (0, 1), (1, 0)):
                        last = down_part(i, j, f, h, w, f == 0 and (h, w) == (0, 0), f == FT - 1 and h == 1)
                last.then_inc(down_done, 1)

            def body(i, r, last):
                if not last:
                    turn_y(i + 1, 1 - r)
                up(i, r)
                if not last:
                    project_out(i + 1)
                down_first(i)
                down(i, 1)
                if not last:
                    turn_x(i + 1, 1 - r)
                down(i, 3)

            pe.wait_ge(id_done, 1)
            turn_y(0, 0)
            pe.wait_ge(ld_wo, 32)
            project_out(0)
            turn_x(0, 0)
            pe.wait_ge(f_lo, 2)
            pe.wait_ge(f_hi, 2)
            body(0, 0, False)
            with pe.Fori(0, B // 2 - 1) as pair:
                body(pair * 2 + 1, 1, False)
                body(pair * 2 + 2, 0, False)
            body(B - 1, 1, True)

        @block.vector
        def _(dve):
            links = [0]

            def link(ins):
                links[0] += 1
                ins.then_inc(vlink, 1)
                dve.wait_ge(vlink, links[0])

            def pow2(dst, inv, src, tmp):
                link(nc.vector.tensor_scalar(tmp, src, 1e-12, None, ALU.max))
                link(nc.vector.tensor_scalar(tmp.bitcast(I32), tmp.bitcast(I32), 0x7F800000, None, ALU.bitwise_and))
                link(nc.vector.tensor_scalar(dst.bitcast(I32), tmp.bitcast(I32), -1.0, float(268 << 23),
                                             ALU.mult, ALU.add))
                link(nc.vector.tensor_scalar(inv.bitcast(I32), dst.bitcast(I32), -1.0, float(254 << 23),
                                             ALU.mult, ALU.add))

            nc.vector.memset(T[HP:P].rearrange("p k c a n -> p (k c a) n")[:, :, 0:HP], 0.0).then_inc(t_zero, 1)
            link(nc.vector.memset(st[:, :], 0.0))
            dve.wait_ge(ld_k, 64)
            for c in range(2):
                tap0 = k_st[:, c, :, 0:1].rearrange("p t o -> p (t o)")
                link(nc.vector.tensor_tensor(tap0, tap0, kd_st[:, c], ALU.add))

            def max_abs(dst, src, axis=AX.XY):
                link(nc.vector.tensor_reduce(dst, src, axis, ALU.max, apply_absolute_value=True))

            def max_of_row_sums(col, src, n):
                link(nc.vector.tensor_reduce(tmp1[:, 0:n], src, AX.X, ALU.add, apply_absolute_value=True))
                max_abs(st[:, col:col + 1], tmp1[:, 0:n], AX.X)

            for c in range(2):
                max_abs(st[:, cK1 + c:cK1 + c + 1], k_st[:, c])
            max_of_row_sums(cL1, k_st[:, 0], DT)
            dve.wait_ge(ld_w, 48)
            max_abs(st[:, cW:cW + 1], w_st)
            max_of_row_sums(cLK, wn_st[:, 0], DT)
            max_of_row_sums(cLV, wn_st[:, 1], DT)
            dve.wait_ge(ld_b, 16)
            for col, s in ((cBK, 0), (cBV, 1)):
                max_abs(st[:, col:col + 1], bias_b[:, :, s])
            dve.wait_ge(vlink, links[0])
            nc.vector.tensor_copy(st[:, NST:NST + 1], st[:, 0:1]).then_inc(st_done, 1)
            dve.wait_ge(gm_done, 1)
            pow2(s1[:, 0:3], i1[:, 0:3], gm[:, 0:3], tmp1[:, 0:3])
            nc.vector.memset(st[:, cF:cF + 3], 0.0).then_inc(scales1, 1)
            for c in range(2):
                dve.wait_ge(kpad_hi, c + 1)
                nc.vector.scalar_tensor_tensor(ksplit[:, c, :, 1], k_st[:, c], s1[:, cK1 + c:cK1 + c + 1],
                                               ksplit[:, c, :, 0], ALU.mult, ALU.subtract).then_inc(kpad_lo, 1)
            for n in range(NU):
                dve.wait_ge(ld_u[n], 16)
                max_abs(um[:, n:n + 1], ust[:, :, n * UP:(n + 1) * UP])
                if n == 0:
                    dve.wait_ge(w_hi, 1)
                    nc.vector.scalar_tensor_tensor(w16[:, :, 1], w_st, s1[:, cW:cW + 1], w16[:, :, 0],
                                                   ALU.mult, ALU.subtract).then_inc(w_lo, 1)
            nc.vector.tensor_reduce(um[:, NU:NU + 1], um[:, 0:NU], AX.X, ALU.max).then_inc(um_done, 1)
            dve.wait_ge(gu_done, 1)
            link(nc.vector.tensor_copy(m2[:, 0:1], gu[:, :]))
            link(nc.vector.tensor_scalar(tmp1[:, 0:1], gu[:, :], gm[:, cLV:cLV + 1], gm[:, cBV:cBV + 1],
                                         ALU.mult, ALU.add))
            link(nc.vector.tensor_scalar(m2[:, 1:2], gu[:, :], gm[:, cLK:cLK + 1], gm[:, cBK:cBK + 1],
                                         ALU.mult, ALU.add))
            link(nc.vector.tensor_scalar(m2[:, 2:3], m2[:, 1:2], gm[:, cL1:cL1 + 1], tmp1[:, 0:1],
                                         ALU.mult, ALU.mult))
            pow2(s2[:, :], i2[:, :], m2[:, 0:3], tmp1[:, 0:3])
            uw = al[:, 1:2]
            link(nc.vector.tensor_tensor(uw, i2[:, 0:1], i1[:, cW:cW + 1], ALU.mult))
            nc.vector.tensor_tensor(al[:, 0:1], uw, s2[:, 1:2], ALU.mult)
            link(nc.vector.tensor_scalar(tmp1[:, 0:1], s2[:, 2:3], i2[:, 1:2], i1[:, cK1:cK1 + 1], ALU.mult, ALU.mult))
            link(nc.vector.tensor_tensor(al[:, 2:3], tmp1[:, 0:1], uw, ALU.mult))
            nc.vector.tensor_scalar(al[:, 3:4], i2[:, 2:3], i1[:, cK2:cK2 + 1], uw, ALU.mult, ALU.mult)
            nc.vector.tensor_scalar(bias_b[:, :, 1:3], bias_b[:, :, 1:3], s2[:, 0:1], s1[:, cW:cW + 1],
                                    ALU.mult, ALU.mult)
            nc.vector.tensor_scalar(bias_b[:, :, 0], bias_b[:, :, 0], s2[:, 1:2], None, ALU.mult
                                    ).then_inc(scales2, 1)
            dve.wait_ge(scales2, 1)

            def split_u(n):
                dve.wait_ge(u_hi, n + 1)
                cols = slice(n * UP, (n + 1) * UP)
                nc.vector.scalar_tensor_tensor(u16[:, 1, :, cols], ust[:, :, cols], s2[:, 0:1], u16[:, 0, :, cols],
                                               ALU.mult, ALU.subtract).then_inc(u_lo, 1)

            def read_projection(quarter, r, n, chunk):
                dve.wait_ge(proj, n + 1)
                if not isinstance(n, int) or n >= 2:
                    dve.wait_ge(k_lo, n - 1)
                tiles = PA.rearrange("p b (i x) -> p (b i) x", i=NI)
                kt = ktmp[:, quarter % 2].rearrange("p (m d) -> p m d", d=CH)
                for s, dst in ((0, kt), (1, quarter_of(vbuf[:, r], quarter)),
                               (2, quarter_of(qy[:, bass.ds(chunk * CH * COL, CH * COL)], quarter))):
                    bb = bias_b[:, bass.ds(chunk, 1), s].to_broadcast([P, 4 * NI, CH])
                    src = tiles[:, :, s * CH:(s + 1) * CH]
                    if s == 0:
                        nc.vector.scalar_tensor_tensor(dst, src, al[:, 0:1], bb, ALU.mult, ALU.add
                                                       ).then_inc(ktmp_ready, 1)
                    else:
                        last = nc.vector.tensor_tensor(dst, src.rearrange("p (b i) d -> p b i d", i=NI),
                                                       bb.rearrange("p (b i) d -> p b i d", i=NI), ALU.add)
                last.then_inc(proj_read, 1)

            def mask(conv, s, g, half):
                slot = 4 + half if conv else s % 2 * 2 + half
                dve.wait_ge(t_in[slot], 16 * (g + 1) if conv else 8 * (g - s % 2) + 16)
                tri = T[0:HP, slot].rearrange("p c a n -> p (c a) n")[:, :, 0:HP]
                nc.vector.tensor_tensor(tri, tri, causal[0:HP, 0:HP].unsqueeze(1).to_broadcast([HP, 2 * HG, HP]),
                                        ALU.mult).then_inc((c1_masked, c2_masked)[conv], 1)

            def windows1(s, g):
                for half in range(2):
                    mask(0, s, g, half)

            def windows2(s, g):
                for half in range(2):
                    mask(1, s, g, half)
                for half in range(2):
                    dve.wait_ge(c2_masked, 2 * g + half + 1)
                    nc.vector.tensor_copy(*shifted(4 + half)).then_inc(c2_copied, 1)

            dve.wait_ge(id_done, 2)
            dve.wait_ge(t_zero, 1)
            windows1(0, 0)
            for quarter in range(GPC):
                for n in range(quarter * NU // GPC, (quarter + 1) * NU // GPC):
                    split_u(n)
                if quarter == 0:
                    dve.wait_ge(u_lo, 2)
                if quarter:
                    read_projection(quarter - 1, 0, quarter - 1, 0)
            read_projection(GPC - 1, 0, GPC - 1, 0)

            def times_v(s, g, n):
                dve.wait_ge(c1_half, 2 * g + 2)
                dve.wait_ge(proj_read, n)
                v = vbuf[:, s // GPC, group_of(s):group_of(s) + GC]
                nc.vector.scalar_tensor_tensor(v, PC1[:, s % 2], al[:, 2:3], v, ALU.mult, ALU.mult
                                               ).then_inc(kv_ready, 1)

            def times_q(s, g):
                dve.wait_ge(c2_half, 2 * g + 2)
                q = qy[:, bass.ds(g * GC, GC)]
                nc.vector.scalar_tensor_tensor(q, PC2[:, s % 2], al[:, 3:4], q, ALU.mult, ALU.mult
                                               ).then_inc(y_ready, 1)

            def step(s, base, more, chunk, first=False):
                g = base + s
                if not (first and s < 2):
                    times_q((s - 2) % PAIR, g - 2)
                if not (isinstance(base, int) and g == NG - 1):
                    windows1((s + 1) % PAIR, g + 1)
                if not (first and s == 0):
                    windows2(s, g - 1)
                if more:
                    if s % GPC == 0 and not (first and s == 0):
                        dve.wait_ge(kv_lo, g)
                    read_projection(s % GPC, (s // GPC + 1) % 2, g + GPC, chunk + s // GPC + 1)
                times_v(s, g, base + (s // GPC + 1) * GPC)

            for s in range(PAIR):
                step(s, 0, True, 0, True)
            with dve.Fori(1, NC // 2 - 1) as pair:
                for s in range(PAIR):
                    step(s, pair * PAIR, True, pair * 2)
            for s in range(PAIR):
                step(s, NG - PAIR, s < GPC, NC - 2)
                if s == PAIR - 2:
                    dve.wait_ge(ld_f, 48)
                    max_abs(st[:, cF:cF + 1], wf_st)
            max_abs(st[:, cP:cP + 1], wp_st)
            dve.wait_ge(squares, FT)
            max_abs(tmp1[:, 0:1], tmp1[:, 8:16], AX.X)
            nc.vector.tensor_scalar(st[:, cH:cH + 1], tmp1[:, 0:1], float(D) * 1.001, None, ALU.mult
                                    ).then_inc(st2_done, 1)
            windows2(0, NG - 1)
            times_q(PAIR - 2, NG - 2)
            dve.wait_ge(gm2_done, 1)
            pow2(s1[:, 3:6], i1[:, 3:6], gm[:, 3:6], tmp1[:, 0:3])
            b32 = srh[:, :].bitcast(I32)
            link(nc.vector.tensor_scalar(b32, s1[:, cH:cH + 1].bitcast(I32), 1, None, ALU.logical_shift_right))
            link(nc.vector.tensor_scalar(b32, b32, float(127 << 22), None, ALU.add))
            link(nc.vector.tensor_scalar(b32, b32, 0x7F800000, None, ALU.bitwise_and))
            link(nc.vector.tensor_scalar(al[:, 4:5], srh[:, :], i1[:, cF:cF + 1], 1.0 / X1S, ALU.mult, ALU.mult))
            link(nc.vector.tensor_scalar(tmp1[:, 0:1], srh[:, :], srh[:, :], s1[:, cP:cP + 1], ALU.mult, ALU.mult))
            for n, edge in enumerate(theta):
                last = nc.vector.tensor_scalar(th[:, n:n + 1], tmp1[:, 0:1], edge, None, ALU.mult)
            last.then_inc(scales3, 1)
            times_q(PAIR - 1, NG - 1)
            dve.wait_ge(f_hi, 1)
            nc.vector.scalar_tensor_tensor(wf16[:, 1], wf_st, s1[:, cF:cF + 1], wf16[:, 0],
                                           ALU.mult, ALU.subtract).then_inc(f_lo, 1)
            dve.wait_ge(f_hi, 2)
            nc.vector.scalar_tensor_tensor(wp16[:, 1], wp_st, s1[:, cP:cP + 1], wp16[:, 0],
                                           ALU.mult, ALU.subtract).then_inc(f_lo, 1)


            def norm_factors(half, i, src):
                dve.wait_ge((sum_ready, sum2_ready)[half], i + 1)
                for j in range(NI):
                    last = nc.vector.bn_stats(bst[:, half, j], src[:, j])
                last.then_inc(moments[half], 1)
                dve.wait_ge(moments[half], i + 1)
                nc.vector.memset(cell[:, half:half + 1], 0.0)
                for j in range(NI):
                    last = nc.vector.bn_aggr(mv[:, half, j], bst[:, half, j])
                last.then_inc((r_ready, x2_ready)[half], 1)

            def norm_shift(half, i):
                dve.wait_ge((rs_ready, rs2_ready)[half], i + 1)
                nc.vector.scalar_tensor_tensor(nm[:, half], mv[:, half, :, 0], -1.0, rs[:, half], ALU.mult, ALU.mult
                                               ).then_inc((nm_ready, nm2_ready)[half], 1)

            def first_sum(i, r):
                dve.wait_ge(wo_done, i + 1)
                dve.wait_ge(ub_ready, i + 1)
                if not isinstance(i, int) or i >= 1:
                    dve.wait_ge(x1_ready, i)
                nc.vector.tensor_tensor(rb.rearrange("p i n -> p (i n)"), PW.rearrange("p a n -> p (a n)"),
                                        ub[:, r].rearrange("p i n -> p (i n)"), ALU.add).then_inc(sum_ready, 1)
                norm_factors(0, i, rb)
                norm_shift(0, i)

            def split_x(i, r):
                dve.wait_ge(x_hi, i + 1)
                nc.vector.scalar_tensor_tensor(x16[:, r, 1], PT, X1S, x16[:, r, 0], ALU.mult, ALU.subtract
                                               ).then_inc(x_lo, 1)

            def square(i, f):
                dve.wait_ge(rl_ready, i * FT + f + 1)
                if not (isinstance(i, int) and i == 0 and f < 4):
                    dve.wait_ge(h_lo, i * FT + f - 3)
                nc.vector.tensor_tensor(hh[:, f % 4], rl[:, f], rl[:, f], ALU.mult).then_inc(hh_ready, 1)

            def spikes(i, half, edges):
                dve.wait_ge(down_done, i * 2 + half + 1)
                y, c = PD[:, half], cnt[:, half * 512:(half + 1) * 512]
                for n in edges:
                    if n == 0:
                        ins = nc.vector.tensor_scalar(c, y, th[:, 0:1], None, ALU.is_gt)
                    else:
                        dve.wait_ge(stair, i * STAIRS + half * len(theta) + n)
                        ins = nc.vector.scalar_tensor_tensor(c, y, th[:, n:n + 1], c, ALU.is_gt, ALU.add)
                    ins.then_inc(stair, 1)

            def second_sum(i, r, first):
                dve.wait_ge(stair, i * STAIRS + STAIRS)
                if not first:
                    dve.wait_ge(ob_ready, i)
                nc.vector.scalar_tensor_tensor(x2.rearrange("p i n -> p (i n)"), cnt, 1.0 / len(theta),
                                               x1[:, r].rearrange("p i n -> p (i n)"), ALU.mult, ALU.add
                                               ).then_inc(sum2_ready, 1)
                norm_factors(1, i, x2)

            first_sum(0, 0)
            split_x(0, 0)

            def body(i, r, first, last):
                for f in range(FT):
                    square(i, f)
                    if f == 0 and not first:
                        norm_shift(1, i - 1)
                if not last:
                    first_sum(i + 1, 1 - r)
                spikes(i, 0, range(0, 3))
                if not last:
                    split_x(i + 1, 1 - r)
                spikes(i, 0, range(3, len(theta)))
                spikes(i, 1, range(0, len(theta)))
                second_sum(i, r, first)

            body(0, 0, True, False)
            with dve.Fori(0, B // 2 - 1) as pair:
                body(pair * 2 + 1, 1, False, False)
                body(pair * 2 + 2, 0, False, False)
            body(B - 1, 1, False, True)
            norm_shift(1, B - 1)


def kernel(**inputs):
    import numpy as np
    import concourse.bacc as bacc
    from concourse.bass_utils import run_bass_kernel_spmd

    f = {k[3:]: np.asarray(v) for k, v in inputs.items()}
    u = np.ascontiguousarray(f["attn_u"]).reshape(B * NI, P, D)
    wk, wv, wq = f["attn_Wk"], f["attn_Wv"], f["attn_Wq"]
    wcat = np.stack([w.T.reshape(D, NC, CH) for w in (wk, wv, wq)], axis=2)
    wcat = wcat.reshape(DT, P, NC, 3 * CH).transpose(1, 2, 0, 3).reshape(P, NC, DT * 3 * CH)
    bias = np.stack([f[n].reshape(NC, CH) for n in ("attn_bk", "attn_bv", "attn_bq")], axis=1).reshape(3 * D)
    arrays = {
        "uT": u.reshape(TOK, D).T, "u": u, "wcat": wcat, "wk_n": wk, "wv_n": wv, "bias": bias, "bo": f["attn_bo"],
        "k1": f["attn_k_kernel"], "k2": f["attn_ssm_kernel"], "kd1": f["attn_k_D"], "kd2": f["attn_D"],
        "woT": f["attn_Wo"].T, "wf_n": f["ffn_W_fc"], "wfT": f["ffn_W_fc"].T, "wpT": f["ffn_W_proj"].T,
    }
    nc = bacc.Bacc("TRN2", target_bir_lowering=False, num_devices=1, dynamic_dma_scratch_size=1024)
    ins, args = {}, []
    for name, a in arrays.items():
        ins[f"in_{name}"] = np.ascontiguousarray(a)
        args.append(nc.dram_tensor(f"in_{name}", a.shape, mybir.dt.from_np(a.dtype), kind="ExternalInput").ap())
    args.append(nc.dram_tensor("out", (B * NI, P, D), F32, kind="ExternalOutput").ap())
    build(nc, *args)
    r = run_bass_kernel_spmd(nc, [ins], core_ids=[0])
    return np.ascontiguousarray(r.results[0]["out"]).reshape(B, L, D)
```

```python
from contextlib import ExitStack

import concourse.bass as bass
from concourse import mybir

ALU = mybir.AluOpType
ACT = mybir.ActivationFunctionType
F32 = mybir.dt.float32
F16 = mybir.dt.float16
BF16 = mybir.dt.bfloat16
I32 = mybir.dt.int32
AX = mybir.AxisListType

P = 128
B, L, D, F = 16, 512, 256, 1024
NI = L // P
DT = D // P
FT = F // P
TOK = B * L
COL = NI * B
CH = 32
NC = D // CH
G = 8
GPC = CH // G
NG = D // G
HG = G // 2
HP = P // 2
ROWS = P + D * 2 * L
NU = 8
UP = TOK // NU
EPS = 1e-5
X1S = 2.0 ** 10

cW, cK1, cK2, cF, cP, cH, cLK, cLV, cBK, cBV, cL1 = range(11)
NST = 11


def spike_thresholds():
    import numpy as np
    one, beta = np.float32(1.0), np.float32(0.9)

    def spikes(bits):
        y = np.array(bits, np.int32).view(np.float32)
        mem, n = np.float32(0.0), 0
        for _ in range(5):
            reset = one if mem > one else np.float32(0.0)
            mem = np.float32(np.float32(np.float32(beta * mem) + y) - reset)
            n += bool(mem > one)
        return n

    found = []
    for n in range(1, 6):
        low, high = 0, int(np.array(4.0, np.float32).view(np.int32))
        while high - low > 1:
            mid = (low + high) // 2
            if spikes(mid) >= n:
                high = mid
            else:
                low = mid
        found.append(float(np.array(low, np.int32).view(np.float32)))
    return found


def build(nc, uT, u, wcat, wk_n, wv_n, bias, bo, k1, k2, kd1, kd2, woT, wfT, wpT, out):
    theta = spike_thresholds()
    STAIRS = 2 * len(theta)
    w16_dram = nc.dram_tensor("w16_dram", [P, NC, 2, DT * 3 * CH], F16, kind="Internal").ap()
    kpad_dram = nc.dram_tensor("kpad_dram", [2, 2, ROWS], F16, kind="Internal").ap()

    with ExitStack() as ctx:
        def sb(name, shape, dt):
            return ctx.enter_context(nc.sbuf_tensor(name, shape, dt))

        def sem(name):
            return ctx.enter_context(nc.semaphore(name))

        qy = sb("qy", [P, D * COL], F32)
        ident = sb("ident", [P, P], F32)
        part_max = sb("part_max", [P, 16], F32)
        all_max = sb("all_max", [P, 16], F32)
        u_maxima = sb("u_maxima", [P, NU + 2], F32)
        u_max = sb("u_max", [P, 1], F32)
        data_max = sb("data_max", [P, 4], F32)
        w_scale = sb("w_scale", [P, 6], F32)
        w_unscale = sb("w_unscale", [P, 6], F32)
        d_scale = sb("d_scale", [P, 3], F32)
        d_unscale = sb("d_unscale", [P, 3], F32)
        relu_scale = sb("relu_scale", [P, 1], F32)
        scratch = sb("scratch", [P, 16], F32)
        read_factor = sb("read_factor", [P, 8], F32)
        stair_at = sb("stair_at", [P, 8], F32)
        cell = sb("cell", [P, 2], F32)
        eps = sb("eps", [P, NI], F32)
        half_neg = sb("half_neg", [P, NI], F32)

        KB = 256
        arena = sb("arena", [P, 628 * KB // 4], F32)
        at = [0]

        def part(kb, dt, pattern=None, **dims):
            a = arena[:, int(at[0]):int(at[0] + kb * KB)]
            at[0] += kb * KB
            if dt != F32:
                a = a.bitcast(dt)
            return a.rearrange(pattern, **dims) if pattern else a

        u16 = part(64, F16, "p (a t n) -> p a t n", a=2, t=DT)
        kv_at = at[0]
        k16 = part(16, F16, "p (r a n) -> p r a n", r=2, a=2)
        vbuf = part(16, F32, "p (r n) -> p r n", r=2)
        wcur = part(1.5, F16, "p (r a t n) -> p r a t n", r=2, a=2, t=DT)
        kv16 = part(4, F16, "p (r a n) -> p r a n", r=2, a=2)
        ktmp = part(4, F32, "p (r n) -> p r n", r=2)
        causal = part(0.25, F16)
        zeros = part(0.25, F16)
        bias_b = part(3, F32, "p (c s d) -> p c s d", c=NC, s=3)
        T = part(6 * 8, F16, "p (k c a n) -> p k c a n", k=6, c=HG, a=2)
        at[0] = 51 * KB
        T2 = part(2 * 8, F16, "p (k c a n) -> p k c a n", k=2, c=HG, a=2)
        at[0] = 0
        w16 = part(6, F16, "p (c a x) -> p c a x", c=NC, a=2)
        at[0] = kv_at
        k_st = part(8, F32, "p (c t n) -> p c t n", c=2, t=DT)
        ksplit = part(8, F16, "p (c t a n) -> p c t a n", c=2, t=DT, a=2)
        w_st = part(6, F32, "p (c x) -> p c x", c=NC)
        wn_st = part(4, F32, "p (c t n) -> p c t n", c=2, t=DT)
        kd_st = part(0.25, F32)[:, 0:2 * DT].rearrange("p (c t) -> p c t", c=2)
        at[0] = 0
        wf16 = part(8, F16, "p (a t n) -> p a t n", a=2, t=DT)
        wp16 = part(8, F16, "p (a t n) -> p a t n", a=2, t=FT)
        wo = part(2, F32, "p (t n) -> p t n", t=DT)
        bo_b = part(1, F32)
        stage_at = at[0]
        wf_st = part(8, F32, "p (t n) -> p t n", t=DT)
        wp_st = part(8, F32, "p (t n) -> p t n", t=FT)
        at[0] = stage_at
        h_square = part(8, F32, "p (r n) -> p r n", r=4)
        h16 = part(16, F16, "p (a f n) -> p a f n", a=2, f=FT)
        yT = part(4, F32, "p (t n) -> p t n", t=DT)
        sum1 = part(4, F32, "p (i n) -> p i n", i=NI)
        u_bo = part(8, F32, "p (r i n) -> p r i n", r=2, i=NI)
        y_seq = part(8, F32, "p (r i n) -> p r i n", r=2, i=NI)
        x1 = part(8, F32, "p (r i n) -> p r i n", r=2, i=NI)
        x16 = part(8, F16, "p (r a t n) -> p r a t n", r=2, a=2, t=DT)
        relu_h = part(16, F32, "p (r n) -> p r n", r=FT)
        spike_count = part(2, BF16)
        x2 = part(4, F32, "p (i n) -> p i n", i=NI)
        out_buf = part(8, F32, "p (r i n) -> p r i n", r=2, i=NI)
        bn_parts = part(0.25, F32)[:, 0:48].rearrange("p (s i n) -> p s i n", s=2, i=NI)
        mean_var = part(0.25, F32)[:, 0:16].rearrange("p (s i n) -> p s i n", s=2, i=NI)
        var_eps = part(0.25, F32)[:, 0:8].rearrange("p (s i) -> p s i", s=2)
        inv_root = part(0.25, F32)[:, 0:8].rearrange("p (s i) -> p s i", s=2)
        neg_mean = part(0.25, F32)[:, 0:8].rearrange("p (s i) -> p s i", s=2)

        ps = ctx.enter_context(nc.psum_tensor("ps", [P, 8, 512], F32))
        PA = ps[:, 0:4, :]
        PAS = (PA, ps[:, 4:8, :])
        PC1 = ps[:, 4:6, :]
        PC2 = ps[:, 6:8, :]
        PT = ps[:, 0:2, :]
        PW = ps[:, 2:4, :]
        PH = ps[:, 4:6, :]
        PD = ps[:, 6:8, :]

        ld_k, ld_w, ld_b, ld_wf, ld_wp, ld_wo = (sem(n) for n in ("ld_k", "ld_w", "ld_b", "ld_wf", "ld_wp", "ld_wo"))
        ld_u = [sem(f"ld_u{n}") for n in range(NU)]
        id_zero, id_done, part_max_done, all_max_done = (
            sem(n) for n in ("id_zero", "id_done", "part_max_done", "all_max_done"))
        u_maxima_done, u_max_done, scales1, scale_u, scales2 = (
            sem(n) for n in ("u_maxima_done", "u_max_done", "scales1", "scale_u", "scales2"))
        part_max2_done, all_max2_done, scales3 = (sem(n) for n in ("part_max2_done", "all_max2_done", "scales3"))
        vlink = sem("vlink")
        w_scaled, w_hi, w_lo, f_hi, f_lo = (sem(n) for n in ("w_scaled", "w_hi", "w_lo", "f_hi", "f_lo"))
        u_hi, u_lo, u_scaled, u_lo_pool = (sem(n) for n in ("u_hi", "u_lo", "u_scaled", "u_lo_pool"))
        kpad_zero, kpad_hi, kpad_lo, kpad_out, w16_out = (
            sem(n) for n in ("kpad_zero", "kpad_hi", "kpad_lo", "kpad_out", "w16_out"))
        t_in = [sem(f"t_in{n}") for n in range(8)]
        t_zero, c1_masked, c2_masked, c1_copied, c2_copied = (
            sem(n) for n in ("t_zero", "c1_masked", "c2_masked", "c1_copied", "c2_copied"))
        c1_copied_dve, c1_half, c2_half = (sem(n) for n in ("c1_copied_dve", "c1_half", "c2_half"))
        ld_wcur = [sem(f"ld_wcur{r}") for r in range(2)]
        proj, proj_read, ktmp_ready, k_hi, k_lo = (sem(n) for n in ("proj", "proj_read", "ktmp_ready", "k_hi",
                                                                    "k_lo"))
        kv_ready, kv_hi, kv_lo, y_ready = (sem(n) for n in ("kv_ready", "kv_hi", "kv_lo", "y_ready"))
        ld_u_seq = [sem(f"ld_u_seq{n}") for n in range(2)]
        u_bo_ready, y_seq_ready, y_turned, yT_ready, wo_done = (
            sem(n) for n in ("u_bo_ready", "y_seq_ready", "y_turned", "yT_ready", "wo_done"))
        sum1_ready, moments1_ready, root1_ready, shift1_ready, x1_ready = (
            sem(n) for n in ("sum1_ready", "moments1_ready", "root1_ready", "shift1_ready", "x1_ready"))
        sum2_ready, moments2_ready, root2_ready, shift2_ready, out_ready = (
            sem(n) for n in ("sum2_ready", "moments2_ready", "root2_ready", "shift2_ready", "out_ready"))
        moments = [sem(f"moments{n}") for n in range(2)]
        var_eps_ready = [sem(f"var_eps_ready{n}") for n in range(2)]
        x_turned, x_hi, x_lo, up_done, relu_ready = (
            sem(n) for n in ("x_turned", "x_hi", "x_lo", "up_done", "relu_ready"))
        square_ready, h_hi, h_lo, down_done, stair = (
            sem(n) for n in ("square_ready", "h_hi", "h_lo", "down_done", "stair"))
        stored = [sem(f"stored{n}") for n in range(2)]

        block = ctx.enter_context(nc.Block())
        GC = G * COL
        u_st = qy[:, :].rearrange("p (t n) -> p t n", t=DT)
        y_by_token = qy[:, :].rearrange("p (d i b) -> p i d b", d=D, i=NI)

        POOL_PIECES = (5, 7)

        def quarter_of(a, quarter):
            return a.rearrange("p (d i b) -> p b i d", d=CH, i=NI)[:, 4 * quarter:4 * quarter + 4]

        def dense(a):
            return a.rearrange("p (b i d) -> p b i d", b=4, i=NI)

        def group_of(s):
            return (s % GPC) * GC

        def windows_of(conv, s, half, last=False):
            if conv == 0:
                return T[:, s % 2 * 2 + half]
            return T2[:, half] if last and s >= GPC and s % 2 == 0 else T[:, 4 + half]

        def shifted(windows):
            t = windows.rearrange("p c a n -> p (c a) n")
            return t[HP:P, :, HP:L], t[0:HP, :, 0:L - HP]

        PAIR = 2 * GPC

        def phase1(eng, step):
            with eng.Fori(0, NC // 2 - 1) as pair:
                for s in range(PAIR):
                    step(s, pair * PAIR, True)
            last = (NC // 2 - 1) * PAIR
            for s in range(PAIR):
                step(s, last, s < GPC)

        @block.sync
        def _(sp):
            for c, k in enumerate((k1, k2)):
                sp.dma_start(k_st[:, c], k.rearrange("(t p) n -> p t n", p=P)).then_inc(ld_k, 16)
            sp.dma_start(w_st, wcat).then_inc(ld_w, 16)
            for c, w in enumerate((wk_n, wv_n)):
                sp.dma_start(wn_st[:, c], w.rearrange("(t p) n -> p t n", p=P)).then_inc(ld_w, 16)
            for n in range(NU):
                sp.dma_start(u_st[:, :, n * UP:(n + 1) * UP],
                             uT.rearrange("(t p) n -> p t n", p=P)[:, :, n * UP:(n + 1) * UP]).then_inc(ld_u[n], 16)

            def load_windows(conv, half, g):
                row = HG * 2 * L
                first = kpad_dram[conv, 0, P + (2 * g + half) * row:]
                second_place = conv == 1 and g >= NG - GPC and g % 2 == 0
                slot = 6 + half if second_place else 4 + half if conv else g % 2 * 2 + half
                windows = windows_of(conv, g % PAIR, half, g >= NG - PAIR)
                sp.dma_start(windows[0:HP].rearrange("p c a n -> p (c a n)"),
                             bass.AP(first.tensor, first.offset, [[ROWS - HP // 2, 2], [-1, HP // 2], [1, row]])
                             ).then_inc(t_in[slot], 16)

            def load_w(chunk, r):
                sp.dma_start(wcur[:, r].rearrange("p a t x -> p (a t x)"),
                             w16_dram[:, bass.ds(chunk, 1)].rearrange("p c a x -> p (c a x)")
                             ).then_inc(ld_wcur[r], 16)

            sp.wait_ge(w16_out, 16)
            load_w(0, 0)
            load_w(1, 1)
            sp.wait_ge(kpad_out, 96)
            for conv, g in ((0, 0), (0, 1), (1, 0)):
                for half in range(2):
                    load_windows(conv, half, g)

            def load_windows2(g):
                for half in range(2):
                    if g != NG - GPC:
                        before = g - 1 if g < NG - GPC else g - 2
                        sp.wait_ge(c2_half, 2 * before + half + 1)
                    load_windows(1, half, g)

            for s in range(NG):
                chunk = s // GPC + 2
                if s % GPC == 0 and chunk < NC:
                    sp.wait_ge(proj, GPC * (chunk - 1))
                    load_w(chunk, chunk % 2)
                if s == NG - GPC:
                    sp.wait_ge(c1_half, 2 * s)
                if s >= NG - GPC:
                    load_windows2(s)
                if s + 2 < NG:
                    for half in range(2):
                        sp.wait_ge(c1_half, 2 * s + half + 1)
                        load_windows(0, half, s + 2)
                if 0 < s < NG - GPC:
                    load_windows2(s)
                if s == NG - GPC - 1:
                    sp.wait_ge(proj, GPC * NC)
                if s == NG - 3:
                    sp.dma_start(wf_st, wfT.rearrange("(t p) n -> p t n", p=P)).then_inc(ld_wf, 16)
                if s == NG - 2:
                    sp.dma_start(wp_st, wpT.rearrange("(t p) n -> p t n", p=P)).then_inc(ld_wp, 16)
            sp.dma_start(wo, woT.rearrange("(t p) n -> p t n", p=P)).then_inc(ld_wo, 16)
            sp.dma_start(bo_b[:, 0:D], bo.partition_broadcast(P)).then_inc(ld_wo, 16)

            sp.wait_ge(c2_half, 2 * (NG - 1))

            def load_u(b, r):
                sp.dma_start(u_bo[:, r], u[bass.ds(b * NI, NI)].rearrange("i p n -> p i n")).then_inc(ld_u_seq[r], 16)

            def store(b, r):
                sp.wait_ge(out_ready, b + 1)
                sp.dma_start(out[bass.ds(b * NI, NI)].rearrange("i p n -> p i n"),
                             out_buf[:, r]).then_inc(stored[r], 16)

            load_u(0, 0)
            load_u(1, 1)
            with sp.Fori(0, B // 2 - 1) as pair:
                for r in range(2):
                    b = pair * 2 + r
                    sp.wait_ge(moments1_ready, b + 1)
                    load_u(b + 2, r)
                    store(b, r)
            store(B - 2, 0)
            store(B - 1, 1)
            for r in range(2):
                sp.wait_ge(stored[r], 16 * (B // 2))

        @block.scalar
        def _(act):
            for c, d in enumerate((kd1, kd2)):
                act.dma_start(kd_st[:, c], d.rearrange("(t p) -> p t", p=P),
                              allow_slow_non_contiguous=True).then_inc(ld_k, 16)
            act.dma_start(bias_b.rearrange("p c s d -> p (c s d)"), bias.partition_broadcast(P)).then_inc(ld_b, 16)
            act.wait_ge(scales1, 1)
            nc.scalar.activation(w_st, w_st, ACT.Copy, scale=w_scale[:, cW:cW + 1]).then_inc(w_scaled, 1)
            act.wait_ge(w_scaled, 1)
            nc.scalar.activation(w16[:, :, 0], w_st, ACT.Copy).then_inc(w_hi, 1)
            for c in range(2):
                nc.scalar.activation(k_st[:, c], k_st[:, c], ACT.Copy,
                                     scale=w_scale[:, cK1 + c:cK1 + c + 1]).then_inc(w_scaled, 1)
            for c in range(2):
                act.wait_ge(w_scaled, c + 2)
                nc.scalar.activation(ksplit[:, c, :, 0], k_st[:, c], ACT.Copy).then_inc(kpad_hi, 1)
            act.wait_ge(w_lo, 1)
            act.wait_ge(w_hi, 1)
            act.dma_start(w16_dram, w16).then_inc(w16_out, 16)
            act.wait_ge(kpad_lo, 2)
            act.wait_ge(kpad_hi, 2)
            act.wait_ge(kpad_zero, 1)
            for copy in range(2):
                for c in range(2):
                    act.dma_start(kpad_dram[c, copy, P:].rearrange("(t p n) -> p t n", p=P, t=DT),
                                  ksplit[:, c].rearrange("p t a n -> p t (a n)")).then_inc(kpad_out, 16)
                act.dma_start(kpad_dram[:, copy, 0:P], zeros[0:2, :]).then_inc(kpad_out, 16)
            act.wait_ge(scale_u, 1)
            act.wait_ge(w16_out, 16)
            for n in range(NU):
                piece, hi = u_st[:, :, n * UP:(n + 1) * UP], u16[:, 0, :, n * UP:(n + 1) * UP]
                if n in POOL_PIECES:
                    nc.scalar.activation(piece, piece, ACT.Copy, scale=d_scale[:, 0:1]).then_inc(u_scaled, 1)
                    act.wait_ge(u_scaled, POOL_PIECES.index(n) + 1)
                    nc.scalar.activation(hi, piece, ACT.Copy).then_inc(u_hi, 1)
                else:
                    nc.scalar.activation(hi, piece, ACT.Copy, scale=d_scale[:, 0:1]).then_inc(u_hi, 1)

            def k_part(quarter, r, n):
                act.wait_ge(ktmp_ready, n + 1)
                nc.scalar.activation(quarter_of(k16[:, r, 0], quarter), dense(ktmp[:, quarter % 2]), ACT.Copy
                                     ).then_inc(k_hi, 1)

            def copy_windows(s, g, half):
                act.wait_ge(c1_masked, 2 * g + half + 1)
                nc.scalar.activation(*shifted(windows_of(0, s, half)), ACT.Copy).then_inc(c1_copied, 1)

            def step(s, base, more):
                if not (isinstance(base, int) and base + s == NG - 1):
                    copy_windows(s + 1, base + s + 1, 0)
                    if not (isinstance(base, int) and base + s + 1 >= NG - GPC):
                        copy_windows(s + 1, base + s + 1, 1)
                if more:
                    k_part(s % GPC, (s // GPC + 1) % 2, base + s + GPC)
                act.wait_ge(kv_ready, base + s + 1)
                nc.scalar.activation(kv16[:, s % 2, 0], vbuf[:, s // GPC, group_of(s):group_of(s) + GC], ACT.Copy
                                     ).then_inc(kv_hi, 1)

            act.wait_ge(kpad_out, 96)
            act.wait_ge(w_lo, 1)
            for quarter in range(GPC):
                k_part(quarter, 0, quarter)
                if quarter < 2:
                    copy_windows(0, 0, quarter)
            with act.Fori(0, NC // 2 - 1) as pair:
                for s in range(PAIR):
                    step(s, pair * PAIR, True)
            for s in range(PAIR):
                step(s, NG - PAIR, s < GPC)


            def y_turn(i):
                act.wait_ge(y_turned, i + 1)
                nc.scalar.activation(yT, PT, ACT.Copy).then_inc(yT_ready, 1)

            def norm(half, i, r):
                src, dst = (sum1, x1[:, r]) if half == 0 else (x2, out_buf[:, r])
                act.wait_ge((shift1_ready, shift2_ready)[half], i + 1)
                for j in range(NI):
                    last = nc.scalar.activation(dst[:, j], src[:, j], ACT.Identity, bias=neg_mean[:, half, j:j + 1],
                                                scale=inv_root[:, half, j:j + 1])
                last.then_inc((x1_ready, out_ready)[half], 1)

            def x_turn(i, r):
                act.wait_ge(x_turned, i + 1)
                nc.scalar.activation(x16[:, r, 0], PT, ACT.Copy, scale=X1S).then_inc(x_hi, 1)

            def hidden_relu(i, f):
                act.wait_ge(up_done, i * FT + f + 1)
                if not isinstance(i, int) or i >= 1:
                    act.wait_ge(square_ready, i * FT + f - FT + 1)
                nc.scalar.activation(relu_h[:, f], PH[:, f % 2], ACT.Relu,
                                     scale=read_factor[:, 4:5]).then_inc(relu_ready, 1)

            def hidden_hi(i, f):
                act.wait_ge(square_ready, i * FT + f + 1)
                nc.scalar.activation(h16[:, 0, f], h_square[:, f % 4], ACT.Copy).then_inc(h_hi, 1)

            HI_LAG = 3

            def body(i, r, first, last, turn=None):
                if not first and not last:
                    y_turn(i + 1)
                if not first:
                    act.wait_ge(down_done, i * 2)
                for f in range(FT + HI_LAG):
                    if f < FT:
                        hidden_relu(i, f)
                    if f >= HI_LAG:
                        hidden_hi(i, f - HI_LAG)
                if not first:
                    if turn is not None:
                        act.wait_ge(stored[1 - r], 16 * turn)
                    norm(1, i - 1, 1 - r)
                if not last:
                    norm(0, i + 1, 1 - r)
                    x_turn(i + 1, 1 - r)

            act.wait_ge(y_ready, NG)
            nc.scalar.activation(y_seq[:, 0], y_by_token[:, :, :, 0], ACT.Copy).then_inc(y_seq_ready, 1)
            y_turn(0)
            act.wait_ge(scales3, 1)
            nc.scalar.activation(wf16[:, 0], wf_st, ACT.Copy, scale=w_scale[:, cF:cF + 1]).then_inc(f_hi, 1)
            nc.scalar.activation(wp16[:, 0], wp_st, ACT.Copy, scale=w_scale[:, cP:cP + 1]).then_inc(f_hi, 1)
            y_turn(1)
            norm(0, 0, 0)
            x_turn(0, 0)
            body(0, 0, True, False)
            body(1, 1, False, False)
            body(2, 0, False, False)
            with act.Fori(1, B // 2 - 1) as pair:
                body(pair * 2 + 1, 1, False, False, pair)
                body(pair * 2 + 2, 0, False, False, pair)
            body(B - 1, 1, False, True, B // 2 - 1)
            act.wait_ge(stored[1], 16 * (B // 2 - 1))
            norm(1, B - 1, 1)

        @block.gpsimd
        def _(pool):
            nc.gpsimd.memset(ident[:, :], 0.0).then_inc(id_zero, 1)
            nc.gpsimd.memset(zeros, 0.0).then_inc(kpad_zero, 1)
            nc.gpsimd.memset(causal, 1.0).then_inc(id_zero, 1)
            nc.gpsimd.memset(half_neg[:, :], -0.5).then_inc(id_zero, 1)
            nc.gpsimd.memset(eps[:, :], EPS).then_inc(id_zero, 1)
            pool.wait_ge(id_zero, 4)
            nc.gpsimd.affine_select(out=ident[:, :], in_=ident[:, :], compare_op=ALU.not_equal, fill=1.0,
                                    base=0, pattern=[[-1, P]], channel_multiplier=1).then_inc(id_done, 1)
            nc.gpsimd.affine_select(out=causal, in_=causal, compare_op=ALU.is_ge, fill=0.0,
                                    base=0, pattern=[[1, P]], channel_multiplier=-1).then_inc(id_done, 1)
            pool.wait_ge(part_max_done, 1)
            nc.gpsimd.partition_all_reduce(all_max[:, 0:NST], part_max[:, 0:NST], P, bass.bass_isa.ReduceOp.max
                                           ).then_inc(all_max_done, 1)
            pool.wait_ge(w_hi, 1)
            nc.gpsimd.tensor_tensor(w16[:, :, 1], w_st, w16[:, :, 0], ALU.subtract).then_inc(w_lo, 1)
            for c in range(2):
                pool.wait_ge(kpad_hi, c + 1)
                nc.gpsimd.tensor_tensor(ksplit[:, c, :, 1], k_st[:, c], ksplit[:, c, :, 0], ALU.subtract
                                        ).then_inc(kpad_lo, 1)
            pool.wait_ge(u_maxima_done, 1)
            nc.gpsimd.partition_all_reduce(u_max[:, :], u_maxima[:, NU:NU + 1], P, bass.bass_isa.ReduceOp.max
                                           ).then_inc(u_max_done, 1)

            def k_part(quarter, r, n):
                pool.wait_ge(k_hi, n + 1)
                nc.gpsimd.tensor_tensor(quarter_of(k16[:, r, 1], quarter), dense(ktmp[:, quarter % 2]),
                                        quarter_of(k16[:, r, 0], quarter), ALU.subtract).then_inc(k_lo, 1)

            def step(s, base, more):
                if more:
                    k_part(s % GPC, (s // GPC + 1) % 2, base + s + GPC)
                pool.wait_ge(kv_hi, base + s + 1)
                nc.gpsimd.tensor_tensor(kv16[:, s % 2, 1], vbuf[:, s // GPC, group_of(s):group_of(s) + GC],
                                        kv16[:, s % 2, 0], ALU.subtract).then_inc(kv_lo, 1)

            def split_u(n):
                pool.wait_ge(u_hi, n + 1)
                cols = slice(n * UP, (n + 1) * UP)
                nc.gpsimd.tensor_tensor(u16[:, 1, :, cols], u_st[:, :, cols], u16[:, 0, :, cols], ALU.subtract
                                        ).then_inc(u_lo_pool, 1)

            for n in POOL_PIECES:
                split_u(n)
            for quarter in range(GPC):
                k_part(quarter, 0, quarter)
            phase1(pool, step)
            pool.wait_ge(part_max2_done, 1)
            nc.gpsimd.partition_all_reduce(all_max[:, cF:cF + 3], part_max[:, cF:cF + 3], P,
                                           bass.bass_isa.ReduceOp.max
                                           ).then_inc(all_max2_done, 1)

            def gather(i, r):
                if not isinstance(i, int):
                    pool.wait_ge(y_turned, i - 1)
                one = y_by_token[:, :, :, bass.ds(i, 1)].rearrange("p i d b -> p i (d b)")
                nc.gpsimd.tensor_copy(y_seq[:, r], one).then_inc(y_seq_ready, 1)

            def add_bo(i, r, nth):
                pool.wait_ge(ld_u_seq[r], 16 * nth)
                nc.gpsimd.tensor_tensor(u_bo[:, r], u_bo[:, r],
                                        bo_b[:, 0:D].unsqueeze(1).to_broadcast([P, NI, D]), ALU.add
                                        ).then_inc(u_bo_ready, 1)

            def h_part(i, f):
                pool.wait_ge(h_hi, i * FT + f + 1)
                nc.gpsimd.tensor_tensor(h16[:, 1, f], h_square[:, f % 4], h16[:, 0, f],
                                        ALU.subtract).then_inc(h_lo, 1)

            def root(half, i):
                pool.wait_ge((moments1_ready, moments2_ready)[half], i + 1)
                nc.gpsimd.tensor_tensor(var_eps[:, half], mean_var[:, half, :, 1], eps[:, :], ALU.add
                                        ).then_inc(var_eps_ready[half], 1)
                pool.wait_ge(var_eps_ready[half], i + 1)
                nc.gpsimd.tensor_tensor(inv_root[:, half], var_eps[:, half], half_neg[:, :], ALU.pow
                                        ).then_inc((root1_ready, root2_ready)[half], 1)

            pool.wait_ge(ld_wo, 32)
            add_bo(0, 0, 1)
            pool.wait_ge(y_ready, NG)
            pool.wait_ge(y_seq_ready, 1)
            gather(1, 1)
            root(0, 0)
            add_bo(1, 1, 1)

            def body(i, r, nth, left, first=False):
                for f in range(FT):
                    h_part(i, f)
                    if f == 4 and not first:
                        root(1, i - 1)
                if left:
                    root(0, i + 1)
                if left > 1:
                    gather(i + 2, r)
                    add_bo(i + 2, r, nth)

            body(0, 0, 2, 2, True)
            with pool.Fori(0, B // 2 - 2) as pair:
                body(pair * 2 + 1, 1, pair + 2, 2)
                body(pair * 2 + 2, 0, pair + 3, 2)
            body(B - 3, 1, B // 2, 2)
            body(B - 2, 0, 0, 1)
            body(B - 1, 1, 0, 0)
            root(1, B - 1)

        @block.tensor
        def _(pe):
            def project(quarter, r, n, banks=PA, before=0):
                if not isinstance(n, int) or n > before:
                    pe.wait_ge(proj_read, n - before)
                for b in range(4 * quarter, 4 * quarter + 4):
                    for i in range(NI):
                        o = banks[:, b % 4, i * P:i * P + 3 * CH]
                        tok = b * L + i * P
                        k = 0
                        for t in range(DT):
                            for x, w in ((0, 0), (0, 1), (1, 0)):
                                last = nc.tensor.matmul(o, u16[:, x, t, tok:tok + P],
                                                        wcur[:, r, w, t],
                                                        start=(k == 0), stop=(k == 3 * DT - 1))
                                k += 1
                last.then_inc(proj, 1)

            def convolve(conv, out, data, s, nth, done, final=False):
                for half in range(2):
                    if conv == 0 and isinstance(nth, int) and nth > NG - GPC:
                        pe.wait_ge(*((c1_copied_dve, nth - (NG - GPC)) if half else (c1_copied, nth + NG - GPC)))
                    else:
                        pe.wait_ge((c1_copied, c2_copied)[conv], 2 * nth + half - 1)
                    for c in range(HG):
                        ch = half * HG + c
                        k = 0
                        for delta in range(NI):
                            cols = (NI - delta) * B
                            for tp, xp in ((0, 0), (0, 1), (1, 0)):
                                win = windows_of(conv, s, half, final)[:, c, tp]
                                last = nc.tensor.matmul(out[:, ch * COL + delta * B:(ch + 1) * COL],
                                                        win[:, delta * P:(delta + 1) * P],
                                                        data(xp, ch)[:, 0:cols],
                                                        start=(k == 0), stop=(k == 3 * NI - 1))
                                k += 1
                    last.then_inc(done, 1)

            pe.wait_ge(ld_wcur[0], 16)
            for quarter in range(GPC):
                pieces = (quarter + 1) * NU // GPC
                by_pool = sum(n < pieces for n in POOL_PIECES)
                pe.wait_ge(u_lo, pieces - by_pool)
                if by_pool:
                    pe.wait_ge(u_lo_pool, by_pool)
                project(quarter, 0, quarter, PAS[quarter % 2], 1)

            def conv1(s, g, k_ready):
                pe.wait_ge(k_lo, k_ready)
                if not isinstance(g, int) or g >= 2:
                    pe.wait_ge(kv_ready, g - 1)
                convolve(0, PC1[:, s % 2], lambda a, ch: k16[:, s // GPC, a,
                                                             group_of(s) + ch * COL:group_of(s) + (ch + 1) * COL],
                         s, g + 1, c1_half)

            def conv2(s, g):
                pe.wait_ge(kv_lo, g + 1)
                if not isinstance(g, int) or g >= 2:
                    pe.wait_ge(y_ready, g - 1)
                convolve(1, PC2[:, s % 2], lambda a, ch: kv16[:, s % 2, a, ch * COL:(ch + 1) * COL],
                         s, g + 1, c2_half, isinstance(g, int) and g >= NG - PAIR)

            def step(s, base, more, pair, first=False):
                g = base + s
                if more:
                    if s % GPC == 0:
                        pe.wait_ge(ld_wcur[(s // GPC + 1) % 2], (pair + s // GPC + 1) * 16)
                    project(s % GPC, (s // GPC + 1) % 2, g + GPC, PA, int(first))
                if first:
                    pe.wait_ge(proj_read, GPC)
                conv1(s, g, base + (s // GPC + 1) * GPC)
                if not first:
                    conv2((s - 1) % PAIR, g - 1)

            for s in range(PAIR):
                step(s, 0, True, 0, s == 0)
            with pe.Fori(1, NC // 2 - 1) as pair:
                for s in range(PAIR):
                    step(s, pair * PAIR, True, pair)
            for s in range(PAIR):
                step(s, NG - PAIR, s < GPC, NC // 2 - 1)
            conv2(PAIR - 1, NG - 1)

            def turn(src, done):
                for i in range(NI):
                    for t in range(DT):
                        last = nc.tensor.transpose(PT[:, t, i * P:(i + 1) * P], src[:, i, t * P:(t + 1) * P],
                                                   ident[:, :])
                last.then_inc(done, 1)

            def turn_y(i, r):
                pe.wait_ge(y_seq_ready, i + 1)
                if not isinstance(i, int) or i >= 2:
                    pe.wait_ge(x_lo, i)
                    pe.wait_ge(x_hi, i)
                turn(y_seq[:, r], y_turned)

            def project_out(i):
                pe.wait_ge(yT_ready, i + 1)
                if not isinstance(i, int) or i >= 1:
                    pe.wait_ge(moments1_ready, i)
                for j in range(NI):
                    for t in range(DT):
                        last = nc.tensor.matmul(PW[:, j // 2, (j % 2) * D:(j % 2 + 1) * D],
                                                yT[:, t, j * P:(j + 1) * P],
                                                wo[:, t], start=(t == 0), stop=(t == DT - 1))
                last.then_inc(wo_done, 1)

            def turn_x(i, r):
                pe.wait_ge(x1_ready, i + 1)
                if isinstance(i, int) and i == 0:
                    pe.wait_ge(yT_ready, 2)
                turn(x1[:, r], x_turned)

            def up(i, r):
                pe.wait_ge(x_hi, i + 1)
                pe.wait_ge(x_lo, i + 1)
                for f in range(FT):
                    if not (isinstance(i, int) and i == 0 and f < 2):
                        pe.wait_ge(relu_ready, i * FT + f - 1)
                    k = 0
                    for t in range(DT):
                        for w, x in ((0, 0), (0, 1), (1, 0)):
                            last = nc.tensor.matmul(PH[:, f % 2], wf16[:, w, t, f * P:(f + 1) * P], x16[:, r, x, t],
                                                    start=(k == 0), stop=(k == 3 * DT - 1))
                            k += 1
                    last.then_inc(up_done, 1)

            def down_part(i, j, f, h, w, first, last):
                return nc.tensor.matmul(PD[:, j // 2, (j % 2) * D:(j % 2 + 1) * D],
                                        h16[:, h, f, j * P:(j + 1) * P], wp16[:, w, f], start=first, stop=last)

            def down_first(i):
                if not isinstance(i, int) or i >= 1:
                    pe.wait_ge(stair, i * STAIRS)
                for f in range(FT):
                    pe.wait_ge(h_hi, i * FT + f + 1)
                    for j in (0, 2):
                        for w in range(2):
                            down_part(i, j, f, 0, w, f == 0 and w == 0, False)
                for f in range(FT):
                    pe.wait_ge(h_lo, i * FT + f + 1)
                    for j in (0, 2):
                        down_part(i, j, f, 1, 0, False, f == FT - 1)

            def down(i, j):
                for f in range(FT):
                    for h, w in ((0, 0), (0, 1), (1, 0)):
                        last = down_part(i, j, f, h, w, f == 0 and (h, w) == (0, 0), f == FT - 1 and h == 1)
                last.then_inc(down_done, 1)

            def body(i, r, last):
                if not last and not (isinstance(i, int) and i == 0):
                    turn_y(i + 1, 1 - r)
                up(i, r)
                if not last:
                    project_out(i + 1)
                down_first(i)
                down(i, 1)
                if not last:
                    turn_x(i + 1, 1 - r)
                down(i, 3)

            pe.wait_ge(id_done, 1)
            turn_y(0, 0)
            pe.wait_ge(ld_wo, 32)
            project_out(0)
            turn_y(1, 1)
            turn_x(0, 0)
            pe.wait_ge(f_lo, 2)
            pe.wait_ge(f_hi, 2)
            body(0, 0, False)
            with pe.Fori(0, B // 2 - 1) as pair:
                body(pair * 2 + 1, 1, False)
                body(pair * 2 + 2, 0, False)
            body(B - 1, 1, True)

        @block.vector
        def _(dve):
            links = [0]

            def link(ins):
                links[0] += 1
                ins.then_inc(vlink, 1)
                dve.wait_ge(vlink, links[0])

            def pow2(dst, inv, src, tmp):
                link(nc.vector.tensor_scalar(tmp, src, 1e-12, None, ALU.max))
                link(nc.vector.tensor_scalar(tmp.bitcast(I32), tmp.bitcast(I32), 0x7F800000, None, ALU.bitwise_and))
                link(nc.vector.tensor_scalar(dst.bitcast(I32), tmp.bitcast(I32), -1.0, float(268 << 23),
                                             ALU.mult, ALU.add))
                link(nc.vector.tensor_scalar(inv.bitcast(I32), dst.bitcast(I32), -1.0, float(254 << 23),
                                             ALU.mult, ALU.add))

            nc.vector.memset(T[HP:P].rearrange("p k c a n -> p (k c a) n")[:, :, 0:HP], 0.0).then_inc(t_zero, 1)
            link(nc.vector.memset(part_max[:, :], 0.0))
            dve.wait_ge(ld_k, 64)
            for c in range(2):
                tap0 = k_st[:, c, :, 0:1].rearrange("p t o -> p (t o)")
                link(nc.vector.tensor_tensor(tap0, tap0, kd_st[:, c], ALU.add))

            def max_abs(dst, src, axis=AX.XY):
                link(nc.vector.tensor_reduce(dst, src, axis, ALU.max, apply_absolute_value=True))

            def max_of_row_sums(col, src, n):
                link(nc.vector.tensor_reduce(scratch[:, 0:n], src, AX.X, ALU.add, apply_absolute_value=True))
                max_abs(part_max[:, col:col + 1], scratch[:, 0:n], AX.X)

            for c in range(2):
                max_abs(part_max[:, cK1 + c:cK1 + c + 1], k_st[:, c])
            max_of_row_sums(cL1, k_st[:, 0], DT)
            dve.wait_ge(ld_w, 48)
            max_abs(part_max[:, cW:cW + 1], w_st)
            max_of_row_sums(cLK, wn_st[:, 0], DT)
            max_of_row_sums(cLV, wn_st[:, 1], DT)
            dve.wait_ge(ld_b, 16)
            for col, s in ((cBK, 0), (cBV, 1)):
                max_abs(part_max[:, col:col + 1], bias_b[:, :, s])
            dve.wait_ge(vlink, links[0])
            nc.vector.tensor_copy(part_max[:, NST:NST + 1], part_max[:, 0:1]).then_inc(part_max_done, 1)
            dve.wait_ge(all_max_done, 1)
            pow2(w_scale[:, 0:3], w_unscale[:, 0:3], all_max[:, 0:3], scratch[:, 0:3])
            nc.vector.memset(part_max[:, cF:cF + 3], 0.0).then_inc(scales1, 1)
            for n in range(NU):
                dve.wait_ge(ld_u[n], 16)
                max_abs(u_maxima[:, n:n + 1], u_st[:, :, n * UP:(n + 1) * UP])
            nc.vector.tensor_reduce(u_maxima[:, NU:NU + 1], u_maxima[:, 0:NU], AX.X,
                                    ALU.max).then_inc(u_maxima_done, 1)
            dve.wait_ge(u_max_done, 1)
            pow2(d_scale[:, 0:1], d_unscale[:, 0:1], u_max[:, :], scratch[:, 0:1])
            nc.vector.memset(cell[:, 0:1], 0.0).then_inc(scale_u, 1)
            link(nc.vector.tensor_scalar(scratch[:, 0:1], u_max[:, :], all_max[:, cLV:cLV + 1],
                                         all_max[:, cBV:cBV + 1],
                                         ALU.mult, ALU.add))
            link(nc.vector.tensor_scalar(data_max[:, 1:2], u_max[:, :], all_max[:, cLK:cLK + 1],
                                         all_max[:, cBK:cBK + 1],
                                         ALU.mult, ALU.add))
            link(nc.vector.tensor_scalar(data_max[:, 2:3], data_max[:, 1:2], all_max[:, cL1:cL1 + 1], scratch[:, 0:1],
                                         ALU.mult, ALU.mult))
            pow2(d_scale[:, 1:3], d_unscale[:, 1:3], data_max[:, 1:3], scratch[:, 1:3])
            uw = read_factor[:, 1:2]
            link(nc.vector.tensor_tensor(uw, d_unscale[:, 0:1], w_unscale[:, cW:cW + 1], ALU.mult))
            nc.vector.tensor_tensor(read_factor[:, 0:1], uw, d_scale[:, 1:2], ALU.mult)
            link(nc.vector.tensor_scalar(scratch[:, 0:1], d_scale[:, 2:3], d_unscale[:, 1:2],
                                         w_unscale[:, cK1:cK1 + 1], ALU.mult, ALU.mult))
            link(nc.vector.tensor_tensor(read_factor[:, 2:3], scratch[:, 0:1], uw, ALU.mult))
            nc.vector.tensor_scalar(read_factor[:, 3:4], d_unscale[:, 2:3], w_unscale[:, cK2:cK2 + 1], uw,
                                    ALU.mult, ALU.mult)
            nc.vector.tensor_scalar(bias_b[:, :, 1:3], bias_b[:, :, 1:3], d_scale[:, 0:1], w_scale[:, cW:cW + 1],
                                    ALU.mult, ALU.mult)
            nc.vector.tensor_scalar(bias_b[:, :, 0], bias_b[:, :, 0], d_scale[:, 1:2], None, ALU.mult
                                    ).then_inc(scales2, 1)
            dve.wait_ge(scales2, 1)

            def split_u(n):
                dve.wait_ge(u_hi, n + 1)
                cols = slice(n * UP, (n + 1) * UP)
                nc.vector.scalar_tensor_tensor(u16[:, 1, :, cols], u_st[:, :, cols], d_scale[:, 0:1],
                                               u16[:, 0, :, cols],
                                               ALU.mult, ALU.subtract).then_inc(u_lo, 1)

            def read_projection(quarter, r, n, chunk, banks=PA):
                dve.wait_ge(proj, n + 1)
                if not isinstance(n, int) or n >= 2:
                    dve.wait_ge(k_lo, n - 1)
                tiles = banks.rearrange("p b (i x) -> p (b i) x", i=NI)
                kt = ktmp[:, quarter % 2].rearrange("p (m d) -> p m d", d=CH)
                for s, dst in ((0, kt), (1, quarter_of(vbuf[:, r], quarter)),
                               (2, quarter_of(qy[:, bass.ds(chunk * CH * COL, CH * COL)], quarter))):
                    bb = bias_b[:, bass.ds(chunk, 1), s].to_broadcast([P, 4 * NI, CH])
                    src = tiles[:, :, s * CH:(s + 1) * CH]
                    if s == 0:
                        nc.vector.scalar_tensor_tensor(dst, src, read_factor[:, 0:1], bb, ALU.mult, ALU.add
                                                       ).then_inc(ktmp_ready, 1)
                    else:
                        last = nc.vector.tensor_tensor(dst, src.rearrange("p (b i) d -> p b i d", i=NI),
                                                       bb.rearrange("p (b i) d -> p b i d", i=NI), ALU.add)
                last.then_inc(proj_read, 1)

            def final(g):
                return isinstance(g, int) and g >= NG - PAIR

            def mask(conv, s, g, half):
                if conv == 0:
                    dve.wait_ge(t_in[s % 2 * 2 + half], 8 * (g - s % 2) + 16)
                elif isinstance(g, int) and g >= NG - GPC:
                    nth = (g - (NG - GPC)) // 2 + 1
                    dve.wait_ge(t_in[4 + half] if g % 2 else t_in[6 + half],
                                16 * (NG - GPC + nth if g % 2 else nth))
                else:
                    dve.wait_ge(t_in[4 + half], 16 * (g + 1))
                tri = windows_of(conv, s, half, final(g))[0:HP].rearrange("p c a n -> p (c a) n")[:, :, 0:HP]
                nc.vector.tensor_tensor(tri, tri, causal[0:HP, 0:HP].unsqueeze(1).to_broadcast([HP, 2 * HG, HP]),
                                        ALU.mult).then_inc((c1_masked, c2_masked)[conv], 1)

            def windows1(s, g):
                for half in range(2):
                    mask(0, s, g, half)
                if isinstance(g, int) and g >= NG - GPC:
                    dve.wait_ge(c1_masked, 2 * g + 2)
                    nc.vector.tensor_copy(*shifted(windows_of(0, s, 1))).then_inc(c1_copied_dve, 1)

            def windows2(s, g):
                for half in range(2):
                    mask(1, s, g, half)
                for half in range(2):
                    dve.wait_ge(c2_masked, 2 * g + half + 1)
                    nc.vector.tensor_copy(*shifted(windows_of(1, s, half, final(g)))).then_inc(c2_copied, 1)

            dve.wait_ge(id_done, 2)
            dve.wait_ge(t_zero, 1)
            for quarter in range(GPC):
                for n in range(quarter * NU // GPC, (quarter + 1) * NU // GPC):
                    if n not in POOL_PIECES:
                        split_u(n)
                if quarter == 0:
                    dve.wait_ge(u_lo, 2)
                if quarter == 1:
                    windows1(0, 0)
                if quarter:
                    read_projection(quarter - 1, 0, quarter - 1, 0, PAS[(quarter - 1) % 2])
            read_projection(GPC - 1, 0, GPC - 1, 0, PAS[(GPC - 1) % 2])

            def times_v(s, g, n):
                dve.wait_ge(c1_half, 2 * g + 2)
                dve.wait_ge(proj_read, n)
                v = vbuf[:, s // GPC, group_of(s):group_of(s) + GC]
                nc.vector.scalar_tensor_tensor(v, PC1[:, s % 2], read_factor[:, 2:3], v, ALU.mult, ALU.mult
                                               ).then_inc(kv_ready, 1)

            def times_q(s, g):
                dve.wait_ge(c2_half, 2 * g + 2)
                q = qy[:, bass.ds(g * GC, GC)]
                nc.vector.scalar_tensor_tensor(q, PC2[:, s % 2], read_factor[:, 3:4], q, ALU.mult, ALU.mult
                                               ).then_inc(y_ready, 1)

            def step(s, base, more, chunk, first=False):
                g = base + s
                if not (first and s < 2):
                    times_q((s - 2) % PAIR, g - 2)
                if not (isinstance(base, int) and g == NG - 1):
                    windows1((s + 1) % PAIR, g + 1)
                if not (first and s == 0):
                    windows2((s - 1) % PAIR, g - 1)
                if more:
                    if s % GPC == 0 and not (first and s == 0):
                        dve.wait_ge(kv_lo, g)
                    read_projection(s % GPC, (s // GPC + 1) % 2, g + GPC, chunk + s // GPC + 1)
                times_v(s, g, base + (s // GPC + 1) * GPC)

            for s in range(PAIR):
                step(s, 0, True, 0, True)
            with dve.Fori(1, NC // 2 - 1) as pair:
                for s in range(PAIR):
                    step(s, pair * PAIR, True, pair * 2)
            for s in range(PAIR):
                step(s, NG - PAIR, s < GPC, NC - 2)
                if s == GPC - 1:
                    nc.vector.memset(T2[HP:P].rearrange("p k c a n -> p (k c a) n")[:, :, 0:HP], 0.0
                                     ).then_inc(t_zero, 1)
                    dve.wait_ge(t_zero, 2)
                if s == PAIR - 2:
                    dve.wait_ge(ld_wf, 16)
                    max_abs(part_max[:, cF:cF + 1], wf_st)
            windows2(PAIR - 1, NG - 1)
            dve.wait_ge(ld_wp, 16)
            max_abs(part_max[:, cP:cP + 1], wp_st)
            nc.vector.tensor_scalar(part_max[:, cH:cH + 1], part_max[:, cF:cF + 1], part_max[:, cF:cF + 1],
                                    D * D * 1.001,
                                    ALU.mult, ALU.mult).then_inc(part_max2_done, 1)
            times_q(PAIR - 2, NG - 2)
            times_q(PAIR - 1, NG - 1)
            dve.wait_ge(all_max2_done, 1)
            pow2(w_scale[:, 3:6], w_unscale[:, 3:6], all_max[:, 3:6], scratch[:, 0:3])
            b32 = relu_scale[:, :].bitcast(I32)
            link(nc.vector.tensor_scalar(b32, w_scale[:, cH:cH + 1].bitcast(I32), 1, None, ALU.logical_shift_right))
            link(nc.vector.tensor_scalar(b32, b32, float(127 << 22), None, ALU.add))
            link(nc.vector.tensor_scalar(b32, b32, 0x7F800000, None, ALU.bitwise_and))
            link(nc.vector.tensor_scalar(read_factor[:, 4:5], relu_scale[:, :], w_unscale[:, cF:cF + 1], 1.0 / X1S,
                                         ALU.mult, ALU.mult))
            link(nc.vector.tensor_scalar(scratch[:, 0:1], relu_scale[:, :], relu_scale[:, :],
                                         w_scale[:, cP:cP + 1], ALU.mult, ALU.mult))
            for n, edge in enumerate(theta):
                last = nc.vector.tensor_scalar(stair_at[:, n:n + 1], scratch[:, 0:1], edge, None, ALU.mult)
            last.then_inc(scales3, 1)
            dve.wait_ge(f_hi, 1)
            nc.vector.scalar_tensor_tensor(wf16[:, 1], wf_st, w_scale[:, cF:cF + 1], wf16[:, 0],
                                           ALU.mult, ALU.subtract).then_inc(f_lo, 1)
            dve.wait_ge(f_hi, 2)
            nc.vector.scalar_tensor_tensor(wp16[:, 1], wp_st, w_scale[:, cP:cP + 1], wp16[:, 0],
                                           ALU.mult, ALU.subtract).then_inc(f_lo, 1)


            def norm_factors(half, i, src):
                dve.wait_ge((sum1_ready, sum2_ready)[half], i + 1)
                for j in range(NI):
                    last = nc.vector.bn_stats(bn_parts[:, half, j], src[:, j])
                last.then_inc(moments[half], 1)
                dve.wait_ge(moments[half], i + 1)
                nc.vector.memset(cell[:, half:half + 1], 0.0)
                for j in range(NI):
                    last = nc.vector.bn_aggr(mean_var[:, half, j], bn_parts[:, half, j])
                last.then_inc((moments1_ready, moments2_ready)[half], 1)

            def norm_shift(half, i):
                dve.wait_ge((root1_ready, root2_ready)[half], i + 1)
                nc.vector.scalar_tensor_tensor(neg_mean[:, half], mean_var[:, half, :, 0], -1.0, inv_root[:, half],
                                               ALU.mult, ALU.mult
                                               ).then_inc((shift1_ready, shift2_ready)[half], 1)

            def first_sum(i, r):
                dve.wait_ge(wo_done, i + 1)
                dve.wait_ge(u_bo_ready, i + 1)
                if not isinstance(i, int) or i >= 1:
                    dve.wait_ge(x1_ready, i)
                nc.vector.tensor_tensor(sum1.rearrange("p i n -> p (i n)"), PW.rearrange("p a n -> p (a n)"),
                                        u_bo[:, r].rearrange("p i n -> p (i n)"), ALU.add).then_inc(sum1_ready, 1)
                norm_factors(0, i, sum1)
                norm_shift(0, i)

            def split_x(i, r):
                dve.wait_ge(x_hi, i + 1)
                nc.vector.scalar_tensor_tensor(x16[:, r, 1], PT, X1S, x16[:, r, 0], ALU.mult, ALU.subtract
                                               ).then_inc(x_lo, 1)

            def square(i, f):
                dve.wait_ge(relu_ready, i * FT + f + 1)
                if not (isinstance(i, int) and i == 0 and f < 4):
                    dve.wait_ge(h_lo, i * FT + f - 3)
                nc.vector.tensor_tensor(h_square[:, f % 4], relu_h[:, f], relu_h[:, f],
                                        ALU.mult).then_inc(square_ready, 1)

            def spikes(i, half, edges):
                dve.wait_ge(down_done, i * 2 + half + 1)
                y, c = PD[:, half], spike_count[:, half * 512:(half + 1) * 512]
                for n in edges:
                    if n == 0:
                        ins = nc.vector.tensor_scalar(c, y, stair_at[:, 0:1], None, ALU.is_gt)
                    else:
                        dve.wait_ge(stair, i * STAIRS + half * len(theta) + n)
                        ins = nc.vector.scalar_tensor_tensor(c, y, stair_at[:, n:n + 1], c, ALU.is_gt, ALU.add)
                    ins.then_inc(stair, 1)

            def second_sum(i, r, first):
                dve.wait_ge(stair, i * STAIRS + STAIRS)
                if not first:
                    dve.wait_ge(out_ready, i)
                nc.vector.scalar_tensor_tensor(x2.rearrange("p i n -> p (i n)"), spike_count, 1.0 / len(theta),
                                               x1[:, r].rearrange("p i n -> p (i n)"), ALU.mult, ALU.add
                                               ).then_inc(sum2_ready, 1)
                norm_factors(1, i, x2)

            first_sum(0, 0)
            split_x(0, 0)

            def body(i, r, first, last):
                for f in range(FT):
                    square(i, f)
                    if f == 2 and not first:
                        second_sum(i - 1, 1 - r, isinstance(i, int) and i == 1)
                if not first:
                    norm_shift(1, i - 1)
                if not last:
                    first_sum(i + 1, 1 - r)
                spikes(i, 0, range(0, 3))
                if not last:
                    split_x(i + 1, 1 - r)
                spikes(i, 0, range(3, len(theta)))
                spikes(i, 1, range(0, len(theta)))

            body(0, 0, True, False)
            body(1, 1, False, False)
            body(2, 0, False, False)
            with dve.Fori(1, B // 2 - 1) as pair:
                body(pair * 2 + 1, 1, False, False)
                body(pair * 2 + 2, 0, False, False)
            body(B - 1, 1, False, True)
            second_sum(B - 1, 1, False)
            norm_shift(1, B - 1)


def kernel(**inputs):
    import numpy as np
    import concourse.bacc as bacc
    from concourse.bass_utils import run_bass_kernel_spmd

    f = {k[3:]: np.asarray(v) for k, v in inputs.items()}
    u = np.ascontiguousarray(f["attn_u"]).reshape(B * NI, P, D)
    wk, wv, wq = f["attn_Wk"], f["attn_Wv"], f["attn_Wq"]
    wcat = np.stack([w.T.reshape(D, NC, CH) for w in (wk, wv, wq)], axis=2)
    wcat = wcat.reshape(DT, P, NC, 3 * CH).transpose(1, 2, 0, 3).reshape(P, NC, DT * 3 * CH)
    bias = np.stack([f[n].reshape(NC, CH) for n in ("attn_bk", "attn_bv", "attn_bq")], axis=1).reshape(3 * D)
    arrays = {
        "uT": u.reshape(TOK, D).T, "u": u, "wcat": wcat, "wk_n": wk, "wv_n": wv, "bias": bias, "bo": f["attn_bo"],
        "k1": f["attn_k_kernel"], "k2": f["attn_ssm_kernel"], "kd1": f["attn_k_D"], "kd2": f["attn_D"],
        "woT": f["attn_Wo"].T, "wfT": f["ffn_W_fc"].T, "wpT": f["ffn_W_proj"].T,
    }
    nc = bacc.Bacc("TRN2", target_bir_lowering=False, num_devices=1, dynamic_dma_scratch_size=1024)
    ins, args = {}, []
    for name, a in arrays.items():
        ins[f"in_{name}"] = np.ascontiguousarray(a)
        args.append(nc.dram_tensor(f"in_{name}", a.shape, mybir.dt.from_np(a.dtype), kind="ExternalInput").ap())
    args.append(nc.dram_tensor("out", (B * NI, P, D), F32, kind="ExternalOutput").ap())
    build(nc, *args)
    r = run_bass_kernel_spmd(nc, [ins], core_ids=[0])
    return np.ascontiguousarray(r.results[0]["out"]).reshape(B, L, D)
```
